# Optimizing a Trainium2 kernel written in Bass

```python
import numpy as np
import jax
import jax.numpy as jnp

def _softmax(x, axis=-1):
    return jax.nn.softmax(x, axis=axis)

def _gelu(x):
    return jax.nn.gelu(x, approximate=True)

def _silu(x):
    return jax.nn.silu(x)

def _sigmoid(x):
    return jax.nn.sigmoid(x)

def _layernorm(x, axis=-1, eps=1e-05):
    m = jnp.mean(x, axis=axis, keepdims=True)
    v = jnp.var(x, axis=axis, keepdims=True)
    return (x - m) / jnp.sqrt(v + eps)

def _scatter_add(tgt, idx, src, axis=0):
    return tgt.at[idx].add(src)

def _segment_sum(src, seg, n):
    return jax.ops.segment_sum(src, seg, n)
kernel_name = 'mk_macaron_d1_jaxref_r8_0c67c9'

def setup_inputs(seed: int=0):
    np.random.seed(seed)
    _w = jnp.asarray

    def _L0_attn_setup():
        import jax, jax.numpy as jnp
        import numpy as np
        BATCH, L, DM, N, R = (2, 256, 128, 16, 64)
        DT_MIN, DT_MAX = (0.001, 0.1)
        key = jax.random.key(seed)
        ks = jax.random.split(key, 6)
        x = jax.random.normal(ks[0], (BATCH, L, DM), jnp.float32)
        W_in = jax.random.normal(ks[1], (DM, 2 * N), jnp.float32) / np.sqrt(DM)
        b_in = jnp.zeros((2 * N,), jnp.float32)
        W_dt1 = jax.random.normal(ks[2], (DM, R), jnp.float32) / np.sqrt(DM)
        b_dt1 = jnp.zeros((R,), jnp.float32)
        dt_std = R ** (-0.5)
        W_dt2 = jax.random.uniform(ks[3], (R, DM), jnp.float32, minval=-dt_std, maxval=dt_std)
        u = jax.random.uniform(ks[4], (DM,), jnp.float32)
        dt0 = jnp.exp(u * (np.log(DT_MAX) - np.log(DT_MIN)) + np.log(DT_MIN))
        b_dt2 = dt0 + jnp.log(-jnp.expm1(-dt0))
        A_row = -(1.0 + jnp.arange(N, dtype=jnp.float32))
        A = jnp.tile(A_row[None, None, None, :], (1, 1, DM, 1))
        D = jnp.ones((DM,), jnp.float32)
        return {'x': x, 'W_in': W_in, 'b_in': b_in, 'W_dt1': W_dt1, 'b_dt1': b_dt1, 'W_dt2': W_dt2, 'b_dt2': b_dt2, 'A': A, 'D': D}
    _L0_attn_in = _L0_attn_setup()

    def _L0_ffn_setup():
        import jax, jax.numpy as jnp
        import numpy as np
        B, T, D = (1, 128, 128)
        E, S, H = (8, 2, 512)
        key = jax.random.key(seed)
        kx, kg, k1, k2, k3 = jax.random.split(key, 5)
        X = jax.random.normal(kx, (B, T, D), jnp.float32)
        Wg = jax.random.normal(kg, (D, E), jnp.float32) * 0.02
        bg = jnp.zeros((E,), jnp.float32)
        W1 = jax.random.normal(k1, (E, D, H), jnp.float32) * 0.02
        W3 = jax.random.normal(k3, (E, D, H), jnp.float32) * 0.02
        W2 = jax.random.normal(k2, (E, H, D), jnp.float32) * 0.02
        return {'X': X, 'Wg': Wg, 'bg': bg, 'W1': W1, 'W2': W2, 'W3': W3}
    _L0_ffn_in = _L0_ffn_setup()
    _d = {'L0_attn_x': _L0_attn_in['x'], 'L0_attn_W_in': _L0_attn_in['W_in'], 'L0_attn_b_in': _L0_attn_in['b_in'], 'L0_attn_W_dt1': _L0_attn_in['W_dt1'], 'L0_attn_b_dt1': _L0_attn_in['b_dt1'], 'L0_attn_W_dt2': _L0_attn_in['W_dt2'], 'L0_attn_b_dt2': _L0_attn_in['b_dt2'], 'L0_attn_A': _L0_attn_in['A'], 'L0_attn_D': _L0_attn_in['D'], 'L0_ffn_Wg': _L0_ffn_in['Wg'], 'L0_ffn_bg': _L0_ffn_in['bg'], 'L0_ffn_W1': _L0_ffn_in['W1'], 'L0_ffn_W2': _L0_ffn_in['W2'], 'L0_ffn_W3': _L0_ffn_in['W3']}
    _x0 = _d['L0_attn_x']
    _d['L0_attn_x'] = jax.random.normal(jax.random.fold_in(jax.random.key(seed), 1), (4, 1024, 128), dtype=_x0.dtype)
    del _x0
    return _d

def reference(L0_attn_x, L0_attn_W_in, L0_attn_b_in, L0_attn_W_dt1, L0_attn_b_dt1, L0_attn_W_dt2, L0_attn_b_dt2, L0_attn_A, L0_attn_D, L0_ffn_Wg, L0_ffn_bg, L0_ffn_W1, L0_ffn_W2, L0_ffn_W3):

    def _L0_attn_ref(x, W_in, b_in, W_dt1, b_dt1, W_dt2, b_dt2, A, D):
        import jax, jax.numpy as jnp
        import numpy as np
        BATCH, L, DM, N, R = (2, 256, 128, 16, 64)
        DT_MIN, DT_MAX = (0.001, 0.1)
        BC = x @ W_in + b_in
        Bm, Cm = (BC[..., :N], BC[..., N:])
        dt = jax.nn.softplus((x @ W_dt1 + b_dt1) @ W_dt2 + b_dt2)
        dt = jnp.clip(dt, 1e-07, 1000000.0)
        tmp = A * dt[..., None]
        A_bar = jnp.exp(tmp)
        B_barX = jnp.expm1(tmp) / tmp * dt[..., None] * Bm[:, :, None, :] * x[..., None]

        def combine(e1, e2):
            a1, b1 = e1
            a2, b2 = e2
            return (a1 * a2, a2 * b1 + b2)
        _, h = jax.lax.associative_scan(combine, (A_bar, B_barX), axis=1)
        return jnp.sum(h * Cm[:, :, None, :], axis=-1) + D * x

    def _L0_ffn_ref(X, Wg, bg, W1, W2, W3):
        import jax, jax.numpy as jnp
        import numpy as np
        B, T, D = (1, 128, 128)
        E, S, H = (8, 2, 512)
        logits = jnp.einsum('btd,de->bte', X, Wg) + bg
        topv, topi = jax.lax.top_k(logits, S)
        w = jax.nn.softmax(topv, axis=-1)
        xs = X[:, :, None, :] * w[..., None]
        out = X
        for e in range(E):
            h = jax.nn.silu(jnp.einsum('btsd,dh->btsh', xs, W1[e])) * jnp.einsum('btsd,dh->btsh', xs, W3[e])
            y = jnp.einsum('btsh,hd->btsd', h, W2[e])
            mask = (topi == e)[..., None]
            out = out + jnp.where(mask, y, 0.0).sum(axis=2)
        return out
    x = L0_attn_x
    x = x + 0.5 * _L0_ffn_ref(_layernorm(x, axis=-1), L0_ffn_Wg, L0_ffn_bg, L0_ffn_W1, L0_ffn_W2, L0_ffn_W3)
    x = x + _L0_attn_ref(_layernorm(x, axis=-1), L0_attn_W_in, L0_attn_b_in, L0_attn_W_dt1, L0_attn_b_dt1, L0_attn_W_dt2, L0_attn_b_dt2, L0_attn_A, L0_attn_D)
    x = x + 0.5 * _L0_ffn_ref(_layernorm(x, axis=-1), L0_ffn_Wg, L0_ffn_bg, L0_ffn_W1, L0_ffn_W2, L0_ffn_W3)
    return x

_drawn_inputs = setup_inputs


def setup_inputs(seed=0):
    import zlib

    import numpy as np

    out = dict(_drawn_inputs(seed))
    spreads = {'L0_attn_b_in': (0.0, 0.8),
     'L0_attn_b_dt1': (0.0, 2.0),
     'L0_attn_D': (1.0, 0.2),
     'L0_ffn_bg': (0.0, 0.8)}
    factors = {'L0_ffn_Wg': 8.0, 'L0_ffn_W1': 8.0, 'L0_ffn_W2': 8.0, 'L0_ffn_W3': 8.0}
    for name, (base, spread) in spreads.items():
        noise = np.random.default_rng([zlib.crc32(name.encode()), seed]).standard_normal(out[name].shape)
        drawn = base * np.exp(spread * noise) if base else spread * noise
        out[name] = jnp.asarray(drawn.astype(out[name].dtype))
    for name, factor in factors.items():
        out[name] = (out[name] * factor).astype(out[name].dtype)
    return out
```

```python
import concourse.bass as bass
from concourse import mybir
from contextlib import ExitStack

F32 = mybir.dt.float32
I32 = mybir.dt.int32
ALU = mybir.AluOpType
ACT = mybir.ActivationFunctionType
AX = mybir.AxisListType

P = 128
D = 128
SEQS, L = 4, 1024
T = SEQS * L
NT = T // P
TS = L // P
N = 16
R = 64
E, H = 8, 512
HC = H // P
S = 2
KT = S * T // P + E
BANK = 512
QN = T // BANK
EPS = 1e-5
BIG = 3.0e38
TINY = 1e-30
DT_MIN, DT_MAX = 1e-7, 1e6


def counter(eng, sem, start=0):
    n = [start]

    def link(ins):
        n[0] = n[0] + 1
        ins.then_inc(sem, 1)
        eng.wait_ge(sem, n[0])
    return link, n


def macaron(nc, x, W_in, b_in, W_dt1, b_dt1, W_dt2, b_dt2, A, Dp, Wg, bg, W1, W2, W3, out):
    xn_dram = nc.dram_tensor("xn_dram", (T, D), F32).ap()
    y_dram = nc.dram_tensor("y_dram", (S * T + KT * P, D), F32).ap()

    with ExitStack() as whole:
        def sb(name, shape, dt=F32):
            return whole.enter_context(nc.sbuf_tensor(name, shape, dt))

        X = sb("X", [P, NT, D])
        XN = sb("XN", [P, NT, D])
        XT = sb("XT", [D, T])
        W1s = sb("W1s", [D, E * H])
        W3s = sb("W3s", [D, E * H])
        W2s = sb("W2s", [P, E * HC * D])
        ident = sb("ident", [P, P])
        ones = sb("ones", [P, P])
        before = sb("before", [P, P])
        Wgs = sb("Wgs", [D, E])
        bgB = sb("bgB", [P, E])
        W_ins = sb("W_ins", [D, 2 * N])
        b_inB = sb("b_inB", [P, 2 * N])
        W_dt1s = sb("W_dt1s", [D, R])
        b_dt1c = sb("b_dt1c", [R, 1])
        W_dt2s = sb("W_dt2s", [R, D])
        b_dt2c = sb("b_dt2c", [D, 1])
        As = sb("As", [D, N])
        Dc = sb("Dc", [D, 1])
        Ahalf = sb("Ahalf", [D, N])
        Ainv = sb("Ainv", [D, N])
        ids = sb("ids", [P, S, NT])
        rev = sb("rev", [P, E])
        iotaR = sb("iotaR", [P, P])
        iotaK = sb("iotaK", [P, KT])
        padrow = sb("padrow", [P, KT])
        notfirst = sb("notfirst", [P, E, NT])
        W = dict(locals())

        load_and_constants(nc, W)
        for layer in range(2):
            normalise(nc, W, f"n{layer}")
            with ExitStack() as ffn:
                def tb(name, shape, dt=F32):
                    return ffn.enter_context(nc.sbuf_tensor(f"{name}_{layer}", shape, dt))
                W["rowG"] = tb("rowG", [P, KT], I32)
                W["rowY"] = tb("rowY", [P, KT], I32)
                W["wpos"] = tb("wpos", [P, KT])
                W["expertW"] = tb("expertW", [P, KT], I32)
                route(nc, W, layer)
                experts(nc, W, layer)
                combine(nc, W, layer)
            if layer == 0:
                normalise(nc, W, "nm")
                with nc.sbuf_tensor("DT", [D, T], F32) as DT:
                    W["DT"] = DT
                    steps(nc, W)
                    scan(nc, W)


def load_and_constants(nc, W):
    with ExitStack() as c:
        loaded = c.enter_context(nc.semaphore("loaded"))
        made = c.enter_context(nc.semaphore("made"))
        dv = c.enter_context(nc.semaphore("dv_c"))
        block = c.enter_context(nc.Block())
        small = [(W["Wgs"], W["Wg"]), (W["bgB"], W["bg"].partition_broadcast(P)),
                 (W["W_ins"], W["W_in"]), (W["b_inB"], W["b_in"].partition_broadcast(P)),
                 (W["W_dt1s"], W["W_dt1"]), (W["W_dt2s"], W["W_dt2"]),
                 (W["b_dt1c"], W["b_dt1"].rearrange("(r a) -> r a", a=1)),
                 (W["b_dt2c"], W["b_dt2"].rearrange("(r a) -> r a", a=1)),
                 (W["As"], W["A"].rearrange("a b d n -> (a b d) n")),
                 (W["Dc"], W["Dp"].rearrange("(r a) -> r a", a=1))]

        @block.sync
        def _(sp):
            sp.dma_start(W["X"][:, :, :], W["x"].rearrange("b (i p) d -> p (b i) d", p=P)).then_inc(loaded, 16)
            for dst, src in small:
                sp.dma_start(dst[:, :], src).then_inc(loaded, 16)
            sp.dma_start(W["W1s"][:, :].rearrange("d (e h) -> d e h", e=E),
                         W["W1"].rearrange("e d h -> d e h")).then_inc(loaded, 16)
            sp.dma_start(W["W3s"][:, :].rearrange("d (e h) -> d e h", e=E),
                         W["W3"].rearrange("e d h -> d e h")).then_inc(loaded, 16)
            sp.dma_start(W["W2s"][:, :].rearrange("p (e c d) -> p e c d", e=E, c=HC),
                         W["W2"].rearrange("e (c p) d -> p e c d", p=P)).then_inc(loaded, 16)
            sp.wait_ge(loaded, 16 * (4 + len(small)))

        @block.gpsimd
        def _(pool):
            nc.gpsimd.memset(W["ident"][:, :], 0.0).then_inc(made, 1)
            nc.gpsimd.memset(W["before"][:, :], 1.0).then_inc(made, 1)
            nc.gpsimd.memset(W["ones"][:, :], 1.0)
            pool.wait_ge(made, 2)
            nc.gpsimd.affine_select(out=W["ident"][:, :], in_=W["ident"][:, :], compare_op=ALU.not_equal,
                                    fill=1.0, base=0, pattern=[[-1, P]], channel_multiplier=1)
            nc.gpsimd.affine_select(out=W["before"][:, :], in_=W["before"][:, :], compare_op=ALU.is_gt,
                                    fill=0.0, base=0, pattern=[[1, P]], channel_multiplier=-1)
            nc.gpsimd.iota(W["ids"][:, :, :], pattern=[[T, S], [P, NT]], base=1, channel_multiplier=1,
                           allow_small_or_imprecise_dtypes=True)
            nc.gpsimd.iota(W["rev"][:, :], pattern=[[-1, E]], base=E, channel_multiplier=0,
                           allow_small_or_imprecise_dtypes=True)
            nc.gpsimd.iota(W["iotaR"][:, :], pattern=[[1, P]], base=0, channel_multiplier=0,
                           allow_small_or_imprecise_dtypes=True)
            nc.gpsimd.iota(W["iotaK"][:, :], pattern=[[1, KT]], base=0, channel_multiplier=0,
                           allow_small_or_imprecise_dtypes=True)
            nc.gpsimd.iota(W["padrow"][:, :], pattern=[[P, KT]], base=S * T + 1, channel_multiplier=1,
                           allow_small_or_imprecise_dtypes=True)

        @block.vector
        def _(dve):
            link, _n = counter(dve, dv)
            link(nc.vector.memset(W["notfirst"][:, :, :], 1.0))
            nc.vector.memset(W["notfirst"][:, :, 0:1], 0.0)
            dve.wait_ge(loaded, 16 * (4 + len(small)))
            nc.vector.tensor_scalar(W["Ahalf"][:, :], W["As"][:, :], 0.5, None, ALU.mult)
            nc.vector.reciprocal(W["Ainv"][:, :], W["As"][:, :])


def normalise(nc, W, tag):
    X, XN, XT, ident = W["X"], W["XN"], W["XT"], W["ident"]
    with ExitStack() as c:
        sq = c.enter_context(nc.sbuf_tensor(f"sq_{tag}", [P, NT, D], F32))
        mean = c.enter_context(nc.sbuf_tensor(f"mean_{tag}", [P, NT], F32))
        var = c.enter_context(nc.sbuf_tensor(f"var_{tag}", [P, NT], F32))
        rstd = c.enter_context(nc.sbuf_tensor(f"rstd_{tag}", [P, NT], F32))
        psT = [c.enter_context(nc.psum_tensor(f"psT{j}_{tag}", [P, BANK], F32)) for j in range(4)]
        sem = lambda n: c.enter_context(nc.semaphore(f"{n}_{tag}"))
        dv, centred, squared, var_ready, sd_ready, xn_ready, turned, copied, stored = map(
            sem, "dv centred squared var_ready sd_ready xn_ready turned copied stored".split())
        block = c.enter_context(nc.Block())

        def seq(t, b):
            return t[:, TS * b:TS * (b + 1), :]

        @block.vector
        def _(dve):
            link, _n = counter(dve, dv)
            for b in range(SEQS):
                cols = slice(TS * b, TS * (b + 1))
                link(nc.vector.reduce_sum(mean[:, cols], seq(X, b), axis=AX.X))
                link(nc.vector.tensor_scalar(mean[:, cols], mean[:, cols], 1.0 / D, None, ALU.mult))
                nc.vector.tensor_tensor(seq(XN, b), seq(X, b),
                                        mean[:, cols].unsqueeze(2).to_broadcast([P, TS, D]),
                                        ALU.subtract).then_inc(centred, 1)
            for b in range(SEQS):
                cols = slice(TS * b, TS * (b + 1))
                dve.wait_ge(squared, b + 1)
                link(nc.vector.reduce_sum(var[:, cols], seq(sq, b), axis=AX.X))
                nc.vector.tensor_scalar(var[:, cols], var[:, cols], 1.0 / D, EPS, ALU.mult,
                                        ALU.add).then_inc(var_ready, 1)
            for b in range(SEQS):
                cols = slice(TS * b, TS * (b + 1))
                dve.wait_ge(sd_ready, b + 1)
                link(nc.vector.reciprocal(rstd[:, cols], rstd[:, cols]))
                nc.vector.tensor_tensor(seq(XN, b), seq(XN, b),
                                        rstd[:, cols].unsqueeze(2).to_broadcast([P, TS, D]),
                                        ALU.mult).then_inc(xn_ready, 1)

        @block.scalar
        def _(act):
            for b in range(SEQS):
                act.wait_ge(centred, b + 1)
                nc.scalar.activation(seq(sq, b), seq(XN, b), ACT.Square).then_inc(squared, 1)
            for b in range(SEQS):
                cols = slice(TS * b, TS * (b + 1))
                act.wait_ge(var_ready, b + 1)
                nc.scalar.activation(rstd[:, cols], var[:, cols], ACT.Sqrt).then_inc(sd_ready, 1)
            for q in range(QN):
                act.wait_ge(turned, q + 1)
                nc.scalar.activation(XT[:, q * BANK:(q + 1) * BANK], psT[q % 4][:, :],
                                     ACT.Copy).then_inc(copied, 1)

        @block.tensor
        def _(pe):
            per = BANK // P
            for q in range(QN):
                pe.wait_ge(xn_ready, q // 2 + 1)
                if q >= 4:
                    pe.wait_ge(copied, q - 3)
                for j in range(per):
                    last = nc.tensor.transpose(psT[q % 4][:, j * P:(j + 1) * P], XN[:, q * per + j, :],
                                               ident[:, :])
                last.then_inc(turned, 1)

        @block.sync
        def _(sp):
            if tag == "nm":
                return
            rows = W["xn_dram"].rearrange("(i p) d -> p i d", p=P)
            for b in range(SEQS):
                sp.wait_ge(xn_ready, b + 1)
                sp.dma_start(seq(rows, b), seq(XN, b)).then_inc(stored, 16)
            sp.wait_ge(stored, 16 * SEQS)


def route(nc, W, layer):
    XT, ids, rev = W["XT"], W["ids"], W["rev"]
    CH = 8
    NCH = S * NT // CH
    with ExitStack() as c:
        tb = lambda n, shape, dt=F32: c.enter_context(nc.sbuf_tensor(f"{n}_{layer}", shape, dt))
        lg = tb("lg", [P, NT, E])
        tmp = tb("tmp", [P, NT, E])
        oh = [tb(f"oh{s}", [P, NT, E]) for s in range(S)]
        m = [tb(f"m{s}", [P, NT]) for s in range(S)]
        mq = tb("mq", [P, NT])
        chosen = tb("chosen", [P, E, NT])
        tot = tb("tot", [P, E, NT])
        inc = tb("inc", [P, E, NT])
        pos = tb("pos", [P, E, NT])
        cnt = tb("cnt", [P, E], I32)
        tiles = tb("tiles", [P, E])
        tend = tb("tend", [P, E])
        toff = tb("toff", [P, E])
        w = tb("w", [P, S, NT])
        ppos = tb("ppos", [P, S, NT])
        pint = tb("pint", [P, S, NT], I32)
        pk = tb("pk", [P, S, NT])
        pr = tb("pr", [P, S, NT])
        past = tb("past", [P, KT, E])
        nexp = tb("nexp", [P, KT])
        ohR = tb("ohR", [P, 2, CH, P])
        ohK = tb("ohK", [P, 2, CH, 2, KT])
        vrow = tb("vrow", [P, KT])
        psL = c.enter_context(nc.psum_tensor(f"psL_{layer}", [P, BANK], F32))
        psA = c.enter_context(nc.psum_tensor(f"psA_{layer}", [P, BANK], F32))
        psB = c.enter_context(nc.psum_tensor(f"psB_{layer}", [P, BANK], F32))
        psR = c.enter_context(nc.psum_tensor(f"psR_{layer}", [P, BANK], F32))
        sem = lambda n: c.enter_context(nc.semaphore(f"{n}_{layer}"))
        dv, logits, gap, expd, chosen_ready, ranked, hot, used, sorted_ = map(
            sem, "dvr logits gap expd chosen_ready ranked hot used sorted".split())
        block = c.enter_context(nc.Block())

        @block.tensor
        def _(pe):
            for i in range(NT):
                last = nc.tensor.matmul(psL[:, i * E:(i + 1) * E], XT[:, i * P:(i + 1) * P], W["Wgs"][:, :],
                                        start=True, stop=True)
            last.then_inc(logits, 1)
            pe.wait_ge(chosen_ready, 1)
            flat = chosen[:, :, :].rearrange("p e i -> p (e i)")
            nc.tensor.matmul(psA[:, 0:E * NT], W["before"][:, :], flat, start=True, stop=True)
            nc.tensor.matmul(psB[:, 0:E * NT], W["ones"][:, :], flat, start=True, stop=True).then_inc(ranked, 1)
            for ch in range(NCH):
                pe.wait_ge(hot, ch + 1)
                for j in range(CH):
                    last = nc.tensor.matmul(psR[:, 0:2 * KT], ohR[:, ch % 2, j, :],
                                            ohK[:, ch % 2, j, :, :].rearrange("p a k -> p (a k)"),
                                            start=(ch == 0 and j == 0), stop=(ch == NCH - 1 and j == CH - 1))
                last.then_inc(used, 1)

        @block.scalar
        def _(act):
            act.wait_ge(gap, 1)
            nc.scalar.activation(m[1][:, :], m[1][:, :], ACT.Exp).then_inc(expd, 1)

        @block.vector
        def _(dve):
            link, _n = counter(dve, dv)
            v = nc.vector

            def over_e(t):
                return t.unsqueeze(2).to_broadcast([P, NT, E])
            revB = rev[:, :].unsqueeze(1).to_broadcast([P, NT, E])
            dve.wait_ge(logits, 1)
            link(v.tensor_tensor(lg[:, :, :], psL[:, 0:NT * E].rearrange("p (i e) -> p i e", e=E),
                                 W["bgB"][:, :].unsqueeze(1).to_broadcast([P, NT, E]), ALU.add))
            for s in range(S):
                link(v.reduce_max(m[s][:, :], lg[:, :, :], axis=AX.X))
                link(v.tensor_tensor(tmp[:, :, :], lg[:, :, :], over_e(m[s][:, :]), ALU.is_ge))
                link(v.tensor_tensor(tmp[:, :, :], tmp[:, :, :], revB, ALU.mult))
                link(v.reduce_max(mq[:, :], tmp[:, :, :], axis=AX.X))
                link(v.tensor_tensor(oh[s][:, :, :], revB, over_e(mq[:, :]), ALU.is_equal))
                if s == 0:
                    link(v.scalar_tensor_tensor(lg[:, :, :], oh[0][:, :, :], -BIG, lg[:, :, :],
                                                ALU.mult, ALU.add))
            v.tensor_tensor(chosen[:, :, :].rearrange("p e i -> p i e"), oh[0][:, :, :], oh[1][:, :, :],
                            ALU.add).then_inc(chosen_ready, 1)
            v.tensor_tensor(m[1][:, :], m[1][:, :], m[0][:, :], ALU.subtract).then_inc(gap, 1)
            dve.wait_ge(expd, 1)
            link(v.tensor_scalar(mq[:, :], m[1][:, :], 1.0, None, ALU.add))
            link(v.reciprocal(w[:, 0, :], mq[:, :]))
            link(v.tensor_tensor(w[:, 1, :], w[:, 0, :], m[1][:, :], ALU.mult))
            dve.wait_ge(ranked, 1)
            flat = lambda t: t[:, :, :].rearrange("p e i -> p (e i)")
            link(v.tensor_copy(flat(tot), psB[:, 0:E * NT]))
            link(v.tensor_tensor_scan(flat(inc), flat(W["notfirst"]), flat(tot), 0.0, ALU.mult, ALU.add))
            link(v.tensor_tensor(flat(pos), flat(inc), flat(tot), ALU.subtract))
            link(v.tensor_tensor(flat(pos), flat(pos), psA[:, 0:E * NT], ALU.add))
            link(v.tensor_scalar(cnt[:, :], inc[:, :, NT - 1], float(P - 1), None, ALU.add))
            link(v.tensor_single_scalar(cnt[:, :], cnt[:, :], 7, ALU.arith_shift_right))
            link(v.tensor_copy(tiles[:, :], cnt[:, :]))
            link(v.tensor_tensor_scan(tend[:, :], W["ones"][:, 0:E], tiles[:, :], 0.0, ALU.mult, ALU.add))
            link(v.tensor_tensor(toff[:, :], tend[:, :], tiles[:, :], ALU.subtract))
            link(v.tensor_scalar(toff[:, :], toff[:, :], float(P), None, ALU.mult))
            link(v.tensor_tensor(pos[:, :, :], pos[:, :, :],
                                 toff[:, :].unsqueeze(2).to_broadcast([P, E, NT]), ALU.add))
            for s in range(S):
                link(v.tensor_tensor(tmp[:, :, :], oh[s][:, :, :],
                                     pos[:, :, :].rearrange("p e i -> p i e"), ALU.mult))
                link(v.reduce_sum(ppos[:, s, :], tmp[:, :, :], axis=AX.X))
            link(v.tensor_copy(pint[:, :, :], ppos[:, :, :]))
            link(v.tensor_single_scalar(pint[:, :, :], pint[:, :, :], 7, ALU.arith_shift_right))
            link(v.tensor_copy(pk[:, :, :], pint[:, :, :]))
            link(v.scalar_tensor_tensor(pr[:, :, :], pk[:, :, :], -float(P), ppos[:, :, :], ALU.mult, ALU.add))
            for ch in range(NCH):
                s, i0 = ch // (NT // CH), ch % (NT // CH) * CH
                if ch >= 2:
                    dve.wait_ge(used, ch - 1)
                col = lambda t: t[:, s, i0:i0 + CH].unsqueeze(2)
                iK = W["iotaK"][:, :].unsqueeze(1).to_broadcast([P, CH, KT])
                o = ohK[:, ch % 2, :, :, :]
                v.tensor_tensor(ohR[:, ch % 2, :, :], W["iotaR"][:, :].unsqueeze(1).to_broadcast([P, CH, P]),
                                col(pr).to_broadcast([P, CH, P]), ALU.is_equal)
                link(v.tensor_tensor(o[:, :, 1, :], iK, col(pk).to_broadcast([P, CH, KT]), ALU.is_equal))
                link(v.tensor_tensor(o[:, :, 0, :], o[:, :, 1, :], col(ids).to_broadcast([P, CH, KT]), ALU.mult))
                v.tensor_tensor(o[:, :, 1, :], o[:, :, 1, :], col(w).to_broadcast([P, CH, KT]),
                                ALU.mult).then_inc(hot, 1)
            link(v.tensor_tensor(past[:, :, :], W["iotaK"][:, :].unsqueeze(2).to_broadcast([P, KT, E]),
                                 tend[:, :].unsqueeze(1).to_broadcast([P, KT, E]), ALU.is_ge))
            link(v.reduce_sum(nexp[:, :], past[:, :, :], axis=AX.X))
            v.tensor_scalar(W["expertW"][:, :], nexp[:, :], float(E - 1), None, ALU.min)
            dve.wait_ge(used, NCH)
            v.tensor_copy(W["wpos"][:, :], psR[:, KT:2 * KT])
            link(v.scalar_tensor_tensor(vrow[:, :], psR[:, 0:KT], 0.0, W["padrow"][:, :], ALU.is_equal, ALU.mult))
            link(v.scalar_tensor_tensor(W["rowY"][:, :], psR[:, 0:KT], -1.0, vrow[:, :], ALU.add, ALU.add))
            link(v.tensor_single_scalar(W["rowG"][:, :], W["rowY"][:, :], T - 1, ALU.bitwise_and))


def experts(nc, W, layer):
    J = 8
    LAG = 2
    AHEAD = 2
    rowG, rowY, wpos, expertW = W["rowG"], W["rowY"], W["wpos"], W["expertW"]
    with ExitStack() as c:
        tb = lambda n, shape, dt=F32: c.enter_context(nc.sbuf_tensor(f"{n}_{layer}", shape, dt))
        ps = lambda n: c.enter_context(nc.psum_tensor(f"{n}_{layer}", [P, BANK], F32))
        sem = lambda n: c.enter_context(nc.semaphore(f"{n}_{layer}"))
        xg = [tb(f"xg{j}", [P, D]) for j in range(J)]
        xw = [tb(f"xw{j}", [P, D]) for j in range(2)]
        xT = [tb(f"xT{j}", [D, P]) for j in range(2)]
        sg = [tb(f"sg{j}", [P, H]) for j in range(2)]
        hid = [tb(f"hid{j}", [P, H]) for j in range(2)]
        hT = [tb(f"hT{j}", [P, H]) for j in range(2)]
        yb = [tb(f"yb{j}", [P, D]) for j in range(J)]
        colG = [tb(f"colG{j}", [P, 1], I32) for j in range(J)]
        colY = [tb(f"colY{j}", [P, 1], I32) for j in range(J)]
        psX, psH = ps("psX"), ps("psH")
        passed = sem("passed")
        psG = [ps(f"psG{j}") for j in range(2)]
        psU = [ps(f"psU{j}") for j in range(2)]
        psY = [ps(f"psY{j}") for j in range(2)]
        gathered = [sem(f"gathered{j}") for j in range(J)]
        scattered = [sem(f"scattered{j}") for j in range(J)]
        gcol, ycol, weighted, x_turned, x_copied, up_g, up_u, silu_ready, hid_ready, h_turned, h_copied, \
            y_ready, y_copied = map(sem, ("gcol ycol weighted x_turned x_copied up_g up_u silu_ready hid_ready "
                                          "h_turned h_copied y_ready y_copied").split())
        block = c.enter_context(nc.Block())

        def column(t, k):
            return t[:, bass.ds(k, 1)]

        def turns(eng, step, first, end):
            with eng.Fori(first, end) as turn:
                for j in range(J):
                    step(turn * J + j, j)

        def wait(eng, sem_, k, back):
            if not isinstance(k, int) or k - back >= 0:
                eng.wait_ge(sem_, k - back + 1)

        @block.gpsimd
        def _(pool):
            def gather(k, j):
                wait(pool, weighted, k, J)
                nc.gpsimd.tensor_copy(colG[j][:, :], column(rowG, k)).then_inc(gcol, 1)
                pool.wait_ge(gcol, k + 1)
                pool.sem_inc(passed, 1)
                nc.gpsimd.indirect_dma_start(
                    xg[j][:, :], None, W["xn_dram"], bass.IndirectOffsetOnAxis(ap=colG[j][:, :], axis=0)
                ).then_inc(gathered[j], 16)

            def scatter(k, j):
                wait(pool, y_copied, k, 0)
                nc.gpsimd.tensor_copy(colY[j][:, :], column(rowY, k)).then_inc(ycol, 1)
                pool.wait_ge(ycol, k + 1)
                pool.sem_inc(passed, 1)
                nc.gpsimd.indirect_dma_start(
                    W["y_dram"], bass.IndirectOffsetOnAxis(ap=colY[j][:, :], axis=0), yb[j][:, :], None
                ).then_inc(scattered[j], 16)

            def step(k, j):
                if not isinstance(k, int) or k >= J:
                    scatter(k - J, j)
                gather(k, j)
            for k in range(J):
                step(k, k)
            turns(pool, step, 1, KT // J)
            for k in range(KT - J, KT):
                scatter(k, k % J)
            for j in range(J):
                pool.wait_ge(scattered[j], 16 * (KT // J))

        @block.vector
        def _(dve):
            def weigh(k, j, turn):
                dve.wait_ge(gathered[j], turn * 16 + 16)
                wait(dve, x_turned, k, 2)
                nc.vector.tensor_scalar(xw[j % 2][:, :], xg[j][:, :], column(wpos, k), None,
                                        ALU.mult).then_inc(weighted, 1)

            def multiply(k, j):
                wait(dve, silu_ready, k, 0)
                wait(dve, up_u, k, 0)
                wait(dve, h_turned, k, 2)
                nc.vector.tensor_tensor(hid[j % 2][:, :], sg[j % 2][:, :], psU[j % 2][:, :],
                                        ALU.mult).then_inc(hid_ready, 1)

            def take_y(k, j, turn):
                wait(dve, y_ready, k, 0)
                if not isinstance(k, int) or k >= J:
                    dve.wait_ge(scattered[j], turn * 16)
                nc.vector.tensor_copy(yb[j][:, :], psY[j % 2][:, 0:D]).then_inc(y_copied, 1)

            weigh(0, 0, 0)
            weigh(1, 1, 0)
            for k in range(2 * J):
                weigh(k + AHEAD, (k + AHEAD) % J, (k + AHEAD) // J)
                multiply(k, k % J)
                if k >= LAG:
                    take_y(k - LAG, (k - LAG) % J, (k - LAG) // J)
            with dve.Fori(2, KT // J - 1) as turn:
                for j in range(J):
                    k = turn * J + j
                    weigh(k + AHEAD, (j + AHEAD) % J, turn + (j + AHEAD) // J)
                    multiply(k, j)
                    take_y(k - LAG, (j - LAG) % J, turn + (j - LAG) // J)
            for k in range(KT - J, KT + LAG):
                if k + AHEAD < KT:
                    weigh(k + AHEAD, (k + AHEAD) % J, (k + AHEAD) // J)
                if k < KT:
                    multiply(k, k % J)
                take_y(k - LAG, (k - LAG) % J, (k - LAG) // J)

        @block.scalar
        def _(act):
            def copy_x(k, j):
                wait(act, x_turned, k, 0)
                wait(act, up_u, k, 2)
                nc.scalar.activation(xT[j % 2][:, :], psX[:, 0:P], ACT.Copy).then_inc(x_copied, 1)

            def silu(k, j):
                wait(act, up_g, k, 0)
                wait(act, hid_ready, k, 2)
                nc.scalar.activation(sg[j % 2][:, :], psG[j % 2][:, :], ACT.Silu).then_inc(silu_ready, 1)

            def copy_h(k, j):
                wait(act, h_turned, k, 0)
                wait(act, y_ready, k, 2)
                nc.scalar.activation(hT[j % 2][:, :], psH[:, :], ACT.Copy).then_inc(h_copied, 1)

            def step(k, j):
                inside = not isinstance(k, int)
                if inside or k < KT:
                    silu(k, j)
                if inside or k + AHEAD < KT:
                    copy_x(k + AHEAD, j)
                if inside or k >= 1:
                    copy_h(k - 1, j + 1)
            copy_x(0, 0)
            copy_x(1, 1)
            for k in range(J):
                step(k, k % J)
            turns(act, step, 1, KT // J - 1)
            for k in range(KT - J, KT + 1):
                step(k, k)

        @block.tensor
        def _(pe):
            def turn_x(k, j):
                wait(pe, weighted, k, 0)
                wait(pe, x_copied, k, 1)
                nc.tensor.transpose(psX[:, 0:P], xw[j % 2][:, :], W["ident"][:, :]).then_inc(x_turned, 1)

            def up(k, j):
                e = pe.value_load(expertW[0:1, bass.ds(k, 1)], min_val=0, max_val=E - 1)
                wait(pe, x_copied, k, 0)
                wait(pe, silu_ready, k, 2)
                nc.tensor.matmul(psG[j % 2][:, :], xT[j % 2][:, :], W["W1s"][:, bass.ds(e * H, H)],
                                 start=True, stop=True).then_inc(up_g, 1)
                wait(pe, hid_ready, k, 2)
                nc.tensor.matmul(psU[j % 2][:, :], xT[j % 2][:, :], W["W3s"][:, bass.ds(e * H, H)],
                                 start=True, stop=True).then_inc(up_u, 1)

            def turn_h(k, j):
                wait(pe, hid_ready, k, 0)
                wait(pe, h_copied, k, 1)
                for q in range(HC):
                    last = nc.tensor.transpose(psH[:, q * P:(q + 1) * P], hid[j % 2][:, q * P:(q + 1) * P],
                                               W["ident"][:, :])
                last.then_inc(h_turned, 1)

            def down(k, j):
                e = pe.value_load(expertW[0:1, bass.ds(k, 1)], min_val=0, max_val=E - 1)
                wait(pe, h_copied, k, 0)
                wait(pe, y_copied, k, 2)
                for q in range(HC):
                    last = nc.tensor.matmul(psY[j % 2][:, 0:D], hT[j % 2][:, q * P:(q + 1) * P],
                                            W["W2s"][:, bass.ds(e * (HC * D) + q * D, D)],
                                            start=(q == 0), stop=(q == HC - 1))
                last.then_inc(y_ready, 1)

            def step(k, j):
                inside = not isinstance(k, int)
                if inside or k < KT:
                    up(k, j)
                if inside or k + AHEAD < KT:
                    turn_x(k + AHEAD, j)
                if inside or 1 <= k <= KT:
                    turn_h(k - 1, j + 1)
                if inside or k >= LAG:
                    down(k - LAG, j)
            turn_x(0, 0)
            turn_x(1, 1)
            for k in range(J):
                step(k, k)
            turns(pe, step, 1, KT // J - 1)
            for k in range(KT - J, KT + LAG):
                step(k, k)


def combine(nc, W, layer):
    X, XN = W["X"], W["XN"]
    with ExitStack() as c:
        ya = c.enter_context(nc.sbuf_tensor(f"ya_{layer}", [P, S, NT, D], F32))
        sem = lambda n: c.enter_context(nc.semaphore(f"{n}_{layer}"))
        came = [sem(f"came{b}") for b in range(SEQS)]
        dv, summed, sent = sem("dvc"), sem("summed"), sem("sent")
        block = c.enter_context(nc.Block())

        @block.sync
        def _(sp):
            rows = W["y_dram"][0:S * T, :].rearrange("(s i p) d -> p s i d", s=S, p=P)
            for b in range(SEQS):
                for s in range(S):
                    sp.dma_start(ya[:, s, TS * b:TS * (b + 1), :], rows[:, s, TS * b:TS * (b + 1), :]).then_inc(came[b], 16)
            if layer == 1:
                res = W["out"].rearrange("b (i p) d -> p (b i) d", p=P)
                for b in range(SEQS):
                    sp.wait_ge(summed, b + 1)
                    sp.dma_start(res[:, TS * b:TS * (b + 1), :], X[:, TS * b:TS * (b + 1), :]).then_inc(sent, 16)
                sp.wait_ge(sent, 16 * SEQS)

        @block.vector
        def _(dve):
            link, _n = counter(dve, dv)
            for b in range(SEQS):
                at = slice(TS * b, TS * (b + 1))
                dve.wait_ge(came[b], 16 * S)
                link(nc.vector.tensor_tensor(ya[:, 0, at, :], ya[:, 0, at, :], ya[:, 1, at, :], ALU.add))
                link(nc.vector.tensor_tensor(ya[:, 0, at, :], ya[:, 0, at, :], XN[:, at, :], ALU.add))
                nc.vector.scalar_tensor_tensor(X[:, at, :], ya[:, 0, at, :], 0.5, X[:, at, :], ALU.mult,
                                               ALU.add).then_inc(summed, 1)


def steps(nc, W):
    XT, DT = W["XT"], W["DT"]
    with ExitStack() as c:
        tb = lambda n, shape: c.enter_context(nc.sbuf_tensor(n, shape, F32))
        ps = lambda n: c.enter_context(nc.psum_tensor(n, [P, BANK], F32))
        sem = lambda n: c.enter_context(nc.semaphore(n))
        rT = tb("rT", [R, T])
        u = tb("u", [D, T])
        lnu = tb("lnu", [D, T])
        den = tb("den", [D, T])
        psr = [ps(f"psr{j}") for j in range(2)]
        psz = [ps(f"psz{j}") for j in range(2)]
        low, low_c, z_done, z_taken, abs_ready, u_ready, ln_ready, dv, av = map(
            sem, "low low_c z_done z_taken abs_ready u_ready ln_ready dvs avs".split())
        block = c.enter_context(nc.Block())
        cut = lambda t, q: t[:, q * BANK:(q + 1) * BANK]

        @block.tensor
        def _(pe):
            for q in range(QN):
                if q >= 2:
                    pe.wait_ge(low_c, q - 1)
                nc.tensor.matmul(psr[q % 2][0:R, :], W["W_dt1s"][:, :], cut(XT, q), start=True,
                                 stop=True).then_inc(low, 1)
                pe.wait_ge(low_c, q + 1)
                if q >= 2:
                    pe.wait_ge(z_taken, q - 1)
                nc.tensor.matmul(psz[q % 2][:, :], W["W_dt2s"][:, :], cut(rT, q), start=True,
                                 stop=True).then_inc(z_done, 1)

        @block.scalar
        def _(act):
            for q in range(QN):
                act.wait_ge(low, q + 1)
                nc.scalar.activation(cut(rT, q), psr[q % 2][0:R, :], ACT.Identity,
                                     bias=W["b_dt1c"][:, :]).then_inc(low_c, 1)
            for q in range(QN):
                act.wait_ge(z_taken, q + 1)
                nc.scalar.activation(cut(u, q), cut(DT, q), ACT.Abs).then_inc(av, 1)
                act.wait_ge(av, q + 1)
                nc.scalar.activation(cut(u, q), cut(u, q), ACT.Exp, scale=-1.0).then_inc(u_ready, 1)
            for q in range(QN):
                act.wait_ge(u_ready, q + 1)
                nc.scalar.activation(cut(lnu, q), cut(u, q), ACT.Ln, bias=1.0).then_inc(ln_ready, 1)

        @block.vector
        def _(dve):
            link, _n = counter(dve, dv)
            v = nc.vector
            for q in range(QN):
                dve.wait_ge(z_done, q + 1)
                v.tensor_scalar(cut(DT, q), psz[q % 2][:, :], W["b_dt2c"][:, :], None, ALU.add).then_inc(z_taken, 1)
            for q in range(QN):
                dve.wait_ge(u_ready, q + 1)
                link(v.tensor_scalar(cut(den, q), cut(u, q), 1.0, -1.0, ALU.add, ALU.add))
                link(v.tensor_scalar(cut(den, q), cut(den, q), TINY, None, ALU.max))
                link(v.reciprocal(cut(den, q), cut(den, q)))
            for q in range(QN):
                dve.wait_ge(ln_ready, q + 1)
                link(v.scalar_tensor_tensor(cut(den, q), cut(lnu, q), TINY, cut(den, q), ALU.max, ALU.mult))
                link(v.tensor_tensor(cut(den, q), cut(den, q), cut(u, q), ALU.mult))
                link(v.scalar_tensor_tensor(cut(DT, q), cut(DT, q), 0.0, cut(den, q), ALU.max, ALU.add))
                link(v.tensor_scalar(cut(DT, q), cut(DT, q), DT_MIN, DT_MAX, ALU.max, ALU.min))


def scan(nc, W):
    XT, DT, X = W["XT"], W["DT"], W["X"]
    M = SEQS * N
    with ExitStack() as c:
        tb = lambda n, shape: c.enter_context(nc.sbuf_tensor(n, shape, F32))
        ps = lambda n, w: c.enter_context(nc.psum_tensor(n, [P, w], F32))
        sem = lambda n: c.enter_context(nc.semaphore(n))
        Wrep = tb("Wrep", [D, 2 * N, P])
        abar = [tb(f"abar{j}", [D, L]) for j in range(2)]
        th = [tb(f"th{j}", [D, L]) for j in range(2)]
        bx = tb("bx", [D, L])
        drive = tb("drive", [D, L])
        h = tb("h", [D, L])
        hc = [tb(f"hc{j}", [D, L]) for j in range(2)]
        yT = tb("yT", [D, L])
        passed = sem("passed")
        psB, psC, psY, psO = ps("psBs", L), ps("psCs", L), ps("psYs", L), ps("psO", L)
        wrep_ready, b_there, b_read, c_there, hc_ready, a_ready, t_ready, dv, h_summed, y_taken, \
            o_turned, o_taken = map(sem, ("wrep_ready b_there b_read c_there hc_ready a_ready t_ready dvm "
                                          "h_summed y_taken o_turned o_taken").split())
        block = c.enter_context(nc.Block())

        @block.tensor
        def _(pe):
            def spread(dst, col, t0):
                for q in range(L // BANK):
                    last = nc.tensor.matmul(dst[:, q * BANK:(q + 1) * BANK], Wrep[:, col, :],
                                            XT[:, bass.ds(t0 + q * BANK, BANK)], start=True, stop=True)
                return last

            def summed(b, n):
                pe.wait_ge(hc_ready, b * N + (n + 1))
                if n == 0 and not isinstance(b, int):
                    pe.wait_ge(y_taken, b)
                for q in range(L // BANK):
                    last = nc.tensor.matmul(psY[:, q * BANK:(q + 1) * BANK], W["ident"][:, :],
                                            hc[n % 2][:, q * BANK:(q + 1) * BANK], start=(n == 0),
                                            stop=(n == N - 1))
                last.then_inc(h_summed, 1)

            def sequence(b):
                first = isinstance(b, int)
                for n in range(N):
                    if not first or n > 0:
                        pe.wait_ge(b_read, b * N + n)
                    spread(psB, n, b * L).then_inc(b_there, 1)
                    if not first or n > 0:
                        pe.wait_ge(hc_ready, b * N + n)
                    spread(psC, N + n, b * L).then_inc(c_there, 1)
                    if n > 0:
                        summed(b, n - 1)
                summed(b, N - 1)
                pe.wait_ge(y_taken, b + 1)
                if not first:
                    pe.wait_ge(o_taken, b)
                for i in range(TS):
                    last = nc.tensor.transpose(psO[:, i * P:(i + 1) * P], yT[:, i * P:(i + 1) * P], W["ident"][:, :])
                last.then_inc(o_turned, 1)

            pe.wait_ge(wrep_ready, 1)
            sequence(0)
            with pe.Fori(1, SEQS) as b:
                sequence(b)

        @block.scalar
        def _(act):
            def sequence(b):
                first = isinstance(b, int)
                for n in range(N):
                    if not first or n >= 2:
                        act.wait_ge(hc_ready, b * N + (n - 1))
                        act.sem_inc(passed, 1)
                    dts = DT[:, bass.ds(b * L, L)]
                    nc.scalar.activation(abar[n % 2][:, :], dts, ACT.Exp, scale=W["As"][:, n:n + 1]).then_inc(a_ready, 1)
                    nc.scalar.activation(th[n % 2][:, :], dts, ACT.Tanh, scale=W["Ahalf"][:, n:n + 1]).then_inc(t_ready, 1)
            sequence(0)
            with act.Fori(1, SEQS) as b:
                sequence(b)

        @block.vector
        def _(dve):
            link, count = counter(dve, dv)
            v = nc.vector
            v.tensor_copy(Wrep[:, :, :], W["W_ins"][:, :].unsqueeze(2).to_broadcast([D, 2 * N, P])).then_inc(wrep_ready, 1)

            def sequence(b):
                first = isinstance(b, int)
                xs = XT[:, bass.ds(b * L, L)]
                for n in range(N):
                    dve.wait_ge(b_there, b * N + (n + 1))
                    v.scalar_tensor_tensor(bx[:, :], psB[:, :], W["b_inB"][:, n:n + 1], xs, ALU.add,
                                           ALU.mult).then_inc(b_read, 1)
                    dve.wait_ge(a_ready, b * N + (n + 1))
                    dve.wait_ge(t_ready, b * N + (n + 1))
                    v.scalar_tensor_tensor(th[n % 2][:, :], abar[n % 2][:, :], 1.0, th[n % 2][:, :], ALU.add,
                                           ALU.mult).then_inc(dv, 1)
                    dve.wait_ge(dv, b * (3 * N) + (3 * n + 1))
                    dve.wait_ge(b_read, b * N + (n + 1))
                    v.scalar_tensor_tensor(drive[:, :], th[n % 2][:, :], W["Ainv"][:, n:n + 1], bx[:, :], ALU.mult,
                                           ALU.mult).then_inc(dv, 1)
                    dve.wait_ge(dv, b * (3 * N) + (3 * n + 2))
                    v.tensor_tensor_scan(h[:, :], abar[n % 2][:, :], drive[:, :], 0.0, ALU.mult, ALU.add).then_inc(dv, 1)
                    dve.wait_ge(dv, b * (3 * N) + (3 * n + 3))
                    dve.wait_ge(c_there, b * N + (n + 1))
                    if not first or n >= 2:
                        dve.wait_ge(h_summed, b * N + (n - 1))
                    v.scalar_tensor_tensor(hc[n % 2][:, :], psC[:, :], W["b_inB"][:, N + n:N + n + 1], h[:, :],
                                           ALU.add, ALU.mult).then_inc(hc_ready, 1)
                dve.wait_ge(h_summed, b * N + N)
                if not first:
                    dve.wait_ge(o_turned, b)
                v.scalar_tensor_tensor(yT[:, :], xs, W["Dc"][:, :], psY[:, :], ALU.mult, ALU.add).then_inc(y_taken, 1)
                dve.wait_ge(o_turned, b + 1)
                at = X[:, bass.ds(b * TS, TS), :]
                v.tensor_tensor(at, at, psO[:, :].rearrange("p (i d) -> p i d", d=D), ALU.add).then_inc(o_taken, 1)
            sequence(0)
            with dve.Fori(1, SEQS) as b:
                sequence(b)


_INS = ['L0_attn_x', 'L0_attn_W_in', 'L0_attn_b_in', 'L0_attn_W_dt1', 'L0_attn_b_dt1', 'L0_attn_W_dt2',
        'L0_attn_b_dt2', 'L0_attn_A', 'L0_attn_D', 'L0_ffn_Wg', 'L0_ffn_bg', 'L0_ffn_W1', 'L0_ffn_W2', 'L0_ffn_W3']


def kernel(**inputs):
    import numpy as np
    import concourse.bacc as bacc
    from concourse.bass_utils import run_bass_kernel_spmd

    nc = bacc.Bacc("TRN2", target_bir_lowering=False, num_devices=1)
    arrays, args = {}, []
    for name in _INS:
        a = np.ascontiguousarray(inputs[name])
        arrays[f"in_{name}"] = a
        args.append(nc.dram_tensor(f"in_{name}", a.shape, mybir.dt.from_np(a.dtype), kind="ExternalInput").ap())
    shape = inputs['L0_attn_x'].shape
    out = nc.dram_tensor("out_x", shape, F32, kind="ExternalOutput").ap()
    macaron(nc, *args, out)
    r = run_bass_kernel_spmd(nc, [arrays], core_ids=[0])
    return r.results[0]["out_x"]
```

```python
import concourse.bass as bass
from concourse import mybir
from contextlib import ExitStack

F32 = mybir.dt.float32
I32 = mybir.dt.int32
BF16 = mybir.dt.bfloat16
F32R = mybir.dt.float32r
ALU = mybir.AluOpType
ACT = mybir.ActivationFunctionType
AX = mybir.AxisListType

P = 128
D = 128
SEQS, L = 4, 1024
T = SEQS * L
NT = T // P
TS = L // P
N = 16
R = 64
E, H = 8, 512
HC = H // P
S = 2
KT = S * T // P + E
BANK = 512
QN = T // BANK
EPS = 1e-5
BIG = 3.0e38
TINY = 1e-30
DT_MIN, DT_MAX = 1e-7, 1e6


def linker(dve, W):
    def link(ins):
        W["own_steps"] += 1
        ins.then_inc(W["own_step"], 1)
        dve.wait_ge(W["own_step"], W["own_steps"])
    return link


def macaron(nc, x, W_in, b_in, W_dt1, b_dt1, W_dt2, b_dt2, A, Dp, Wg, bg, W1, W2, W3, out):
    xw_dram = nc.dram_tensor("xw_dram", (S * T, D), F32).ap()
    y_dram = nc.dram_tensor("y_dram", (S * T + KT * P, D), F32).ap()

    with ExitStack() as whole:
        def sb(name, shape, dt=F32):
            return whole.enter_context(nc.sbuf_tensor(name, shape, dt))

        X = sb("X", [P, NT, D])
        XN = sb("XN", [P, NT, D])
        XT = sb("XT", [D, T])
        W1h, W1l = sb("W1h", [D, E * H], F32R), sb("W1l", [D, E * H], F32R)
        W3h, W3l = sb("W3h", [D, E * H], F32R), sb("W3l", [D, E * H], F32R)
        W2s = sb("W2s", [P, E * HC * D])
        ident = sb("ident", [P, P])
        ones = sb("ones", [P, P])
        before = sb("before", [P, P])
        Wgs = sb("Wgs", [D, E])
        bgB = sb("bgB", [P, E])
        W_ins = sb("W_ins", [D, 2 * N])
        pick = sb("pick", [3 * 2 * N, 2 * N, P], BF16)
        W_dt1s = sb("W_dt1s", [D, R])
        b_dt1c = sb("b_dt1c", [R, 1])
        W_dt2s = sb("W_dt2s", [R, D])
        b_dt2c = sb("b_dt2c", [D, 1])
        As = sb("As", [D, N])
        Dc = sb("Dc", [D, 1])
        Ahalf = sb("Ahalf", [D, N])
        Ainv = sb("Ainv", [D, N])
        ids = sb("ids", [P, S, NT])
        rev = sb("rev", [P, E])
        iotaR = sb("iotaR", [P, P])
        iotaK = sb("iotaK", [P, KT])
        padrow = sb("padrow", [P, KT])
        notfirst = sb("notfirst", [P, E, NT])
        came = [whole.enter_context(nc.semaphore(f"came{b}")) for b in range(SEQS)]
        small_came = whole.enter_context(nc.semaphore("small_came"))
        w13_came = [whole.enter_context(nc.semaphore(f"w{m}_came")) for m in (1, 3)]
        w2_came = whole.enter_context(nc.semaphore("w2_came"))
        pick_made = whole.enter_context(nc.semaphore("pick_made"))
        own_step = whole.enter_context(nc.semaphore("own_step"))
        own_steps = 0
        W = dict(locals())

        for layer in range(2):
            with ExitStack() as ffn:
                def tb(name, shape, dt=F32):
                    return ffn.enter_context(nc.sbuf_tensor(f"{name}_{layer}", shape, dt))
                W["rowG"] = tb("rowG", [P, KT], I32)
                W["rowY"] = tb("rowY", [P, KT], I32)
                W["expertW"] = tb("expertW", [P, KT], I32)
                with nc.psum_tensor(f"psL_{layer}", [P, BANK], F32) as psL:
                    W["psL"] = psL
                    if layer == 0:
                        with nc.sbuf_tensor("W1raw", [D, E * H], F32) as W1raw, \
                                nc.sbuf_tensor("W3raw", [D, E * H], F32) as W3raw:
                            W["W1raw"], W["W3raw"] = W1raw, W3raw
                            load_and_constants(nc, W)
                            normalise(nc, W, "n0", loads=True, combines=False, scanned=False, gate=True)
                    else:
                        normalise(nc, W, "n1", loads=False, combines=False, scanned=True, gate=True)
                    route(nc, W, layer)
                experts(nc, W, layer)
            if layer == 0:
                normalise(nc, W, "nm", loads=False, combines=True, scanned=False, gate=False)
                with nc.sbuf_tensor("DT", [D, T], F32) as DT, nc.sbuf_tensor("BC3", [3 * 2 * N, T], BF16) as BC3:
                    W["DT"], W["BC3"] = DT, BC3
                    steps(nc, W)
                    scan(nc, W)
        combine(nc, W)


def load_and_constants(nc, W):
    small = [(W["Wgs"], W["Wg"]), (W["bgB"], W["bg"].partition_broadcast(P)),
             (W["W_ins"], W["W_in"]),
             (W["W_dt1s"], W["W_dt1"]), (W["W_dt2s"], W["W_dt2"]),
             (W["b_dt1c"], W["b_dt1"].rearrange("(r a) -> r a", a=1)),
             (W["b_dt2c"], W["b_dt2"].rearrange("(r a) -> r a", a=1)),
             (W["As"], W["A"].rearrange("a b d n -> (a b d) n")),
             (W["Dc"], W["Dp"].rearrange("(r a) -> r a", a=1))]
    W["small_all"] = 16 * len(small)
    with ExitStack() as c:
        made = c.enter_context(nc.semaphore("made"))
        block = c.enter_context(nc.Block())

        @block.sync
        def _(sp):
            for b in range(SEQS):
                sp.dma_start(W["X"][:, b * TS:(b + 1) * TS, :],
                             W["x"][b].rearrange("(i p) d -> p i d", p=P)).then_inc(W["came"][b], 16)
            for dst, src in small:
                sp.dma_start(dst[:, :], src).then_inc(W["small_came"], 16)
            for raw, src, came in ((W["W1raw"], W["W1"], W["w13_came"][0]), (W["W3raw"], W["W3"], W["w13_came"][1])):
                sp.dma_start(raw[:, :].rearrange("d (e h) -> d e h", e=E),
                             src.rearrange("e d h -> d e h")).then_inc(came, 16)
            sp.dma_start(W["W2s"][:, :].rearrange("p (e c d) -> p e c d", e=E, c=HC),
                         W["W2"].rearrange("e (c p) d -> p e c d", p=P)).then_inc(W["w2_came"], 16)

        @block.gpsimd
        def _(pool):
            nc.gpsimd.memset(W["ident"][:, :], 0.0).then_inc(made, 1)
            nc.gpsimd.memset(W["before"][:, :], 1.0).then_inc(made, 1)
            nc.gpsimd.memset(W["ones"][:, :], 1.0)
            pool.wait_ge(made, 2)
            nc.gpsimd.affine_select(out=W["ident"][:, :], in_=W["ident"][:, :], compare_op=ALU.not_equal,
                                    fill=1.0, base=0, pattern=[[-1, P]], channel_multiplier=1)
            nc.gpsimd.affine_select(out=W["before"][:, :], in_=W["before"][:, :], compare_op=ALU.is_gt,
                                    fill=0.0, base=0, pattern=[[1, P]], channel_multiplier=-1)
            nc.gpsimd.iota(W["ids"][:, :, :], pattern=[[T, S], [P, NT]], base=1, channel_multiplier=1,
                           allow_small_or_imprecise_dtypes=True)
            nc.gpsimd.iota(W["rev"][:, :], pattern=[[-1, E]], base=E, channel_multiplier=0,
                           allow_small_or_imprecise_dtypes=True)
            nc.gpsimd.iota(W["iotaR"][:, :], pattern=[[1, P]], base=0, channel_multiplier=0,
                           allow_small_or_imprecise_dtypes=True)
            nc.gpsimd.iota(W["iotaK"][:, :], pattern=[[1, KT]], base=0, channel_multiplier=0,
                           allow_small_or_imprecise_dtypes=True)
            nc.gpsimd.iota(W["padrow"][:, :], pattern=[[P, KT]], base=S * T + 1, channel_multiplier=1,
                           allow_small_or_imprecise_dtypes=True)

        @block.vector
        def _(dve):
            link = linker(dve, W)
            link(nc.vector.memset(W["notfirst"][:, :, :], 1.0))
            nc.vector.memset(W["notfirst"][:, :, 0:1], 0.0)


def normalise(nc, W, tag, loads, combines, scanned, gate):
    per = BANK // P
    X, XN, XT, ident = W["X"], W["XN"], W["XT"], W["ident"]
    with ExitStack() as c:
        tb = lambda n, shape: c.enter_context(nc.sbuf_tensor(f"{n}_{tag}", shape, F32))
        sq = tb("sq", [P, NT, D])
        less = tb("less", [P, NT])
        ssq = tb("ssq", [P, NT])
        rstd = tb("rstd", [P, NT])
        unit = tb("unit", [P, 1])
        ya = tb("ya", [P, S, NT, D]) if combines else None
        psT = [c.enter_context(nc.psum_tensor(f"psT{j}_{tag}", [P, BANK], F32)) for j in range(4)]
        sem = lambda n: c.enter_context(nc.semaphore(f"{n}_{tag}"))
        unit_ready, meaned, squared, var_ready, sd_ready, xn_ready, turned, copied = map(
            sem, "unit_ready meaned squared var_ready sd_ready xn_ready turned copied".split())
        psV = [c.enter_context(nc.psum_tensor(f"psV{j}", [P, BANK], F32)) for j in range(3)] if scanned else None
        y_turned, y_added = (sem("y_turned"), sem("y_added")) if scanned else (None, None)
        block = c.enter_context(nc.Block())

        parts = [(W["W1raw"], W["W1h"], W["W1l"]), (W["W3raw"], W["W3h"], W["W3l"])] if loads else []
        high_made = sem("high_made") if loads else None

        def seq(t, b):
            return t[:, TS * b:TS * (b + 1), :]

        if combines:
            @block.sync
            def _(sp):
                load_outputs(sp, W, ya)

        if loads:
            @block.gpsimd
            def _(pool):
                for m, (raw, high, low) in enumerate(parts):
                    for e in range(E):
                        at = slice(e * H, (e + 1) * H)
                        pool.wait_ge(high_made, m * E + e + 1)
                        nc.gpsimd.tensor_tensor(low[:, at], raw[:, at], high[:, at], ALU.subtract)

        @block.vector
        def _(dve):
            link = linker(dve, W)
            v = nc.vector
            v.memset(unit[:, :], 1.0).then_inc(unit_ready, 1)
            for b in range(SEQS + 1):
                if b < SEQS:
                    cols = slice(TS * b, TS * (b + 1))
                    if loads:
                        dve.wait_ge(W["came"][b], 16)
                    if combines:
                        add_outputs(nc, dve, link, W, ya, 0, b)
                    if scanned:
                        for q in (2 * b, 2 * b + 1):
                            at = X[:, q * per:(q + 1) * per, :]
                            dve.wait_ge(y_turned, q + 1)
                            v.tensor_tensor(at, at, psV[q % 3][:, :].rearrange("p (i d) -> p i d", d=D),
                                            ALU.add).then_inc(y_added, 1)
                        dve.wait_ge(y_added, 2 * b + 2)
                    link(v.reduce_sum(less[:, cols], seq(X, b), axis=AX.X))
                    v.tensor_scalar(less[:, cols], less[:, cols], -1.0 / D, None, ALU.mult).then_inc(meaned, 1)
                if b >= 1:
                    cols = slice(TS * (b - 1), TS * b)
                    dve.wait_ge(squared, NT // SEQS * b)
                    v.tensor_scalar(rstd[:, cols], ssq[:, cols], 1.0 / D, EPS, ALU.mult, ALU.add).then_inc(var_ready, 1)
                    dve.wait_ge(sd_ready, b)
                    link(v.reciprocal(rstd[:, cols], rstd[:, cols]))
                    for i in range(TS * (b - 1), TS * b):
                        v.tensor_scalar(XN[:, i, :], X[:, i, :], less[:, i:i + 1], rstd[:, i:i + 1], ALU.add,
                                        ALU.mult).then_inc(xn_ready, 1)

        @block.scalar
        def _(act):
            def copy_turned(q):
                act.wait_ge(turned, q + 1)
                nc.scalar.activation(XT[:, q * BANK:(q + 1) * BANK], psT[q % 4][:, :],
                                     ACT.Copy).then_inc(copied, 1)

            act.wait_ge(unit_ready, 1)
            nc.scalar.activation(unit[:, :], unit[:, :], ACT.Sqrt)
            for b in range(SEQS + 1):
                if b >= 1:
                    cols = slice(TS * (b - 1), TS * b)
                    act.wait_ge(var_ready, b)
                    nc.scalar.activation(rstd[:, cols], rstd[:, cols], ACT.Sqrt).then_inc(sd_ready, 1)
                if b < SEQS:
                    act.wait_ge(meaned, b + 1)
                    for i in range(TS * b, TS * (b + 1)):
                        nc.scalar.activation(sq[:, i, :], X[:, i, :], ACT.Square, bias=less[:, i:i + 1],
                                             accum_out=ssq[:, i:i + 1]).then_inc(squared, 1)
                if b >= 1:
                    copy_turned(2 * (b - 1))
                    copy_turned(2 * (b - 1) + 1)
                if loads and b in (1, 3):
                    m = b // 2
                    raw, high, _low = parts[m]
                    act.wait_ge(W["w13_came"][m], 16)
                    for e in range(E):
                        at = slice(e * H, (e + 1) * H)
                        nc.scalar.activation(high[:, at], raw[:, at], ACT.Copy).then_inc(high_made, 1)

        @block.tensor
        def _(pe):
            def turn_y(q):
                if q >= 3:
                    pe.wait_ge(y_added, q - 2)
                for j in range(per):
                    last = nc.tensor.transpose(psV[q % 3][:, j * P:(j + 1) * P],
                                               XT[:, (q * per + j) * P:(q * per + j + 1) * P], ident[:, :])
                last.then_inc(y_turned, 1)

            def gates(q):
                pe.wait_ge(copied, q + 1)
                for i in range(q * per, (q + 1) * per):
                    nc.tensor.matmul(W["psL"][:, i * E:(i + 1) * E], XT[:, i * P:(i + 1) * P], W["Wgs"][:, :],
                                     start=True, stop=True)

            if loads:
                pe.wait_ge(W["small_came"], W["small_all"])
            if scanned:
                for q in range(4):
                    turn_y(q)
            for q in range(QN):
                pe.wait_ge(xn_ready, per * (q + 1))
                if q >= 4:
                    pe.wait_ge(copied, q - 3)
                for j in range(per):
                    last = nc.tensor.transpose(psT[q % 4][:, j * P:(j + 1) * P], XN[:, q * per + j, :],
                                               ident[:, :])
                last.then_inc(turned, 1)
                if scanned and q + 4 < QN:
                    turn_y(q + 4)
                if gate and q >= 1:
                    gates(q - 1)
            if gate:
                gates(QN - 1)


def load_outputs(sp, W, ya):
    rows = W["y_dram"][0:S * T, :].rearrange("(s i p) d -> p s i d", s=S, p=P)
    for b in range(SEQS):
        for s in range(S):
            at = slice(TS * b, TS * (b + 1))
            sp.dma_start(ya[:, s, at, :], rows[:, s, at, :]).then_inc(W["came"][b], 16)


def add_outputs(nc, dve, link, W, ya, layer, b):
    at = slice(TS * b, TS * (b + 1))
    X = W["X"]
    dve.wait_ge(W["came"][b], 16 + 16 * S * (layer + 1))
    link(nc.vector.tensor_tensor(ya[:, 0, at, :], ya[:, 0, at, :], ya[:, 1, at, :], ALU.add))
    link(nc.vector.scalar_tensor_tensor(X[:, at, :], ya[:, 0, at, :], 0.5, X[:, at, :], ALU.mult, ALU.add))


def route(nc, W, layer):
    XN, ids, rev, psL = W["XN"], W["ids"], W["rev"], W["psL"]
    CH = 8
    NCH = S * NT // CH
    with ExitStack() as c:
        tb = lambda n, shape, dt=F32: c.enter_context(nc.sbuf_tensor(f"{n}_{layer}", shape, dt))
        lg = tb("lg", [P, NT, E])
        tmp = tb("tmp", [P, NT, E])
        oh = [tb(f"oh{s}", [P, NT, E]) for s in range(S)]
        m = [tb(f"m{s}", [P, NT]) for s in range(S)]
        mq = tb("mq", [P, NT])
        chosen = tb("chosen", [P, E, NT])
        tot = tb("tot", [P, E, NT])
        inc = tb("inc", [P, E, NT])
        pos = tb("pos", [P, E, NT])
        cnt = tb("cnt", [P, E], I32)
        tiles = tb("tiles", [P, E])
        tend = tb("tend", [P, E])
        toff = tb("toff", [P, E])
        w = tb("w", [P, S, NT])
        ppos = tb("ppos", [P, S, NT])
        pint = tb("pint", [P, S, NT], I32)
        pk = tb("pk", [P, S, NT])
        pr = tb("pr", [P, S, NT])
        past = tb("past", [P, KT, E])
        nexp = tb("nexp", [P, KT])
        ohR = tb("ohR", [P, 2, CH, P])
        ohK = tb("ohK", [P, 2, CH, KT])
        xw = tb("xw", [P, S, NT, D])
        vrow = tb("vrow", [P, KT])
        psA = c.enter_context(nc.psum_tensor(f"psA_{layer}", [P, BANK], F32))
        psB = c.enter_context(nc.psum_tensor(f"psB_{layer}", [P, BANK], F32))
        psR = c.enter_context(nc.psum_tensor(f"psR_{layer}", [P, BANK], F32))
        sem = lambda n: c.enter_context(nc.semaphore(f"{n}_{layer}"))
        gap, expd, w_ready, xw_ready, xw_stored, chosen_ready, ranked, tile_hot, hot, used = map(
            sem, "gap expd w_ready xw_ready xw_stored chosen_ready ranked tile_hot hot used".split())
        block = c.enter_context(nc.Block())

        @block.tensor
        def _(pe):
            pe.wait_ge(chosen_ready, 1)
            flat = chosen[:, :, :].rearrange("p e i -> p (e i)")
            nc.tensor.matmul(psA[:, 0:E * NT], W["before"][:, :], flat, start=True, stop=True)
            nc.tensor.matmul(psB[:, 0:E * NT], W["ones"][:, :], flat, start=True, stop=True).then_inc(ranked, 1)
            for ch in range(NCH):
                pe.wait_ge(hot, ch + 1)
                for j in range(CH):
                    last = nc.tensor.matmul(psR[:, 0:KT], ohR[:, ch % 2, j, :], ohK[:, ch % 2, j, :],
                                            start=(ch == 0 and j == 0), stop=(ch == NCH - 1 and j == CH - 1))
                last.then_inc(used, 1)

        @block.scalar
        def _(act):
            act.wait_ge(gap, 1)
            nc.scalar.activation(m[1][:, :], m[1][:, :], ACT.Exp).then_inc(expd, 1)
            act.wait_ge(w_ready, 1)
            for s in range(S):
                for i in range(NT):
                    nc.scalar.activation(xw[:, s, i, :], XN[:, i, :], ACT.Copy,
                                         scale=w[:, s, i:i + 1]).then_inc(xw_ready, 1)

        @block.sync
        def _(sp):
            rows = W["xw_dram"].rearrange("(s i p) d -> p s i d", s=S, p=P)
            for s in range(S):
                for b in range(SEQS):
                    at = slice(TS * b, TS * (b + 1))
                    sp.wait_ge(xw_ready, s * NT + TS * (b + 1))
                    sp.dma_start(rows[:, s, at, :], xw[:, s, at, :]).then_inc(xw_stored, 16)
            sp.wait_ge(xw_stored, 16 * S * SEQS)

        if layer == 0:
            @block.gpsimd
            def _(pool):
                nc.gpsimd.memset(W["pick"][:, :, :], 0.0).then_inc(W["pick_made"], 1)
                for g in range(3):
                    pool.wait_ge(W["pick_made"], 1 + g)
                    rows = W["pick"][g * 2 * N:(g + 1) * 2 * N, :, :]
                    nc.gpsimd.affine_select(out=rows, in_=rows, compare_op=ALU.not_equal, fill=1.0, base=0,
                                            pattern=[[-1, 2 * N], [0, P]],
                                            channel_multiplier=1).then_inc(W["pick_made"], 1)

        @block.vector
        def _(dve):
            link = linker(dve, W)
            v = nc.vector

            def over_e(t):
                return t.unsqueeze(2).to_broadcast([P, NT, E])
            revB = rev[:, :].unsqueeze(1).to_broadcast([P, NT, E])
            if layer == 0:
                dve.wait_ge(W["small_came"], W["small_all"])
            link(v.tensor_tensor(lg[:, :, :], psL[:, 0:NT * E].rearrange("p (i e) -> p i e", e=E),
                                 W["bgB"][:, :].unsqueeze(1).to_broadcast([P, NT, E]), ALU.add))
            for s in range(S):
                link(v.reduce_max(m[s][:, :], lg[:, :, :], axis=AX.X))
                link(v.tensor_tensor(tmp[:, :, :], lg[:, :, :], over_e(m[s][:, :]), ALU.is_ge))
                link(v.tensor_tensor(tmp[:, :, :], tmp[:, :, :], revB, ALU.mult))
                link(v.reduce_max(mq[:, :], tmp[:, :, :], axis=AX.X))
                link(v.tensor_tensor(oh[s][:, :, :], revB, over_e(mq[:, :]), ALU.is_equal))
                if s == 0:
                    link(v.scalar_tensor_tensor(lg[:, :, :], oh[0][:, :, :], -BIG, lg[:, :, :],
                                                ALU.mult, ALU.add))
            v.tensor_tensor(chosen[:, :, :].rearrange("p e i -> p i e"), oh[0][:, :, :], oh[1][:, :, :],
                            ALU.add).then_inc(chosen_ready, 1)
            v.tensor_tensor(m[1][:, :], m[1][:, :], m[0][:, :], ALU.subtract).then_inc(gap, 1)
            dve.wait_ge(expd, 1)
            link(v.tensor_scalar(mq[:, :], m[1][:, :], 1.0, None, ALU.add))
            link(v.reciprocal(w[:, 0, :], mq[:, :]))
            v.tensor_tensor(w[:, 1, :], w[:, 0, :], m[1][:, :], ALU.mult).then_inc(w_ready, 1)
            dve.wait_ge(ranked, 1)
            flat = lambda t: t[:, :, :].rearrange("p e i -> p (e i)")
            link(v.tensor_copy(flat(tot), psB[:, 0:E * NT]))
            link(v.tensor_tensor_scan(flat(inc), flat(W["notfirst"]), flat(tot), 0.0, ALU.mult, ALU.add))
            link(v.tensor_tensor(flat(pos), flat(inc), flat(tot), ALU.subtract))
            link(v.tensor_tensor(flat(pos), flat(pos), psA[:, 0:E * NT], ALU.add))
            link(v.tensor_scalar(cnt[:, :], inc[:, :, NT - 1], float(P - 1), None, ALU.add))
            link(v.tensor_single_scalar(cnt[:, :], cnt[:, :], 7, ALU.arith_shift_right))
            link(v.tensor_copy(tiles[:, :], cnt[:, :]))
            link(v.tensor_tensor_scan(tend[:, :], W["ones"][:, 0:E], tiles[:, :], 0.0, ALU.mult, ALU.add))
            link(v.tensor_tensor(toff[:, :], tend[:, :], tiles[:, :], ALU.subtract))
            link(v.tensor_scalar(toff[:, :], toff[:, :], float(P), None, ALU.mult))
            link(v.tensor_tensor(pos[:, :, :], pos[:, :, :],
                                 toff[:, :].unsqueeze(2).to_broadcast([P, E, NT]), ALU.add))
            for s in range(S):
                link(v.tensor_tensor(tmp[:, :, :], oh[s][:, :, :],
                                     pos[:, :, :].rearrange("p e i -> p i e"), ALU.mult))
                link(v.reduce_sum(ppos[:, s, :], tmp[:, :, :], axis=AX.X))
            link(v.tensor_copy(pint[:, :, :], ppos[:, :, :]))
            link(v.tensor_single_scalar(pint[:, :, :], pint[:, :, :], 7, ALU.arith_shift_right))
            link(v.tensor_copy(pk[:, :, :], pint[:, :, :]))
            link(v.scalar_tensor_tensor(pr[:, :, :], pk[:, :, :], -float(P), ppos[:, :, :], ALU.mult, ALU.add))
            for ch in range(NCH):
                s, i0 = ch // (NT // CH), ch % (NT // CH) * CH
                if ch >= 2:
                    dve.wait_ge(used, ch - 1)
                col = lambda t: t[:, s, i0:i0 + CH].unsqueeze(2)
                iK = W["iotaK"][:, :].unsqueeze(1).to_broadcast([P, CH, KT])
                o = ohK[:, ch % 2, :, :]
                v.tensor_tensor(o, iK, col(pk).to_broadcast([P, CH, KT]), ALU.is_equal).then_inc(tile_hot, 1)
                v.tensor_tensor(ohR[:, ch % 2, :, :], W["iotaR"][:, :].unsqueeze(1).to_broadcast([P, CH, P]),
                                col(pr).to_broadcast([P, CH, P]), ALU.is_equal)
                dve.wait_ge(tile_hot, ch + 1)
                v.tensor_tensor(o, o, col(ids).to_broadcast([P, CH, KT]), ALU.mult).then_inc(hot, 1)
            link(v.tensor_tensor(past[:, :, :], W["iotaK"][:, :].unsqueeze(2).to_broadcast([P, KT, E]),
                                 tend[:, :].unsqueeze(1).to_broadcast([P, KT, E]), ALU.is_ge))
            link(v.reduce_sum(nexp[:, :], past[:, :, :], axis=AX.X))
            v.tensor_scalar(W["expertW"][:, :], nexp[:, :], float(E - 1), None, ALU.min)
            dve.wait_ge(used, NCH)
            link(v.scalar_tensor_tensor(vrow[:, :], psR[:, 0:KT], 0.0, W["padrow"][:, :], ALU.is_equal, ALU.mult))
            link(v.scalar_tensor_tensor(W["rowY"][:, :], psR[:, 0:KT], -1.0, vrow[:, :], ALU.add, ALU.add))
            link(v.tensor_single_scalar(W["rowG"][:, :], W["rowY"][:, :], S * T - 1, ALU.bitwise_and))


def experts(nc, W, layer):
    J = 8
    LAG = 2
    AHEAD = 2
    XCOLS = NT // (2 * J)
    X, XN = W["X"], W["XN"]
    rowG, rowY, expertW = W["rowG"], W["rowY"], W["expertW"]
    with ExitStack() as c:
        tb = lambda n, shape, dt=F32: c.enter_context(nc.sbuf_tensor(f"{n}_{layer}", shape, dt))
        ps = lambda n: c.enter_context(nc.psum_tensor(f"{n}_{layer}", [P, BANK], F32))
        sem = lambda n: c.enter_context(nc.semaphore(f"{n}_{layer}"))
        xg = [tb(f"xg{j}", [P, D]) for j in range(J)]
        xTh = [tb(f"xTh{j}", [D, P], F32R) for j in range(2)]
        xTl = [tb(f"xTl{j}", [D, P], F32R) for j in range(2)]
        sg = [tb(f"sg{j}", [P, H]) for j in range(2)]
        hid = [tb(f"hid{j}", [P, H]) for j in range(2)]
        hT = [tb(f"hT{j}", [P, H]) for j in range(2)]
        yb = [tb(f"yb{j}", [P, D]) for j in range(J)]
        colG = [tb(f"colG{j}", [P, 1], I32) for j in range(J)]
        colY = [tb(f"colY{j}", [P, 1], I32) for j in range(J)]
        psX, psH = ps("psX"), ps("psH")
        passed = sem("passed")
        psG = [ps(f"psG{j}") for j in range(2)]
        psU = [ps(f"psU{j}") for j in range(2)]
        psY = [ps(f"psY{j}") for j in range(2)]
        gathered = [sem(f"gathered{j}") for j in range(J)]
        scattered = [sem(f"scattered{j}") for j in range(J)]
        gcol, ycol, x_turned, x_high, x_low, up_g, up_u, silu_ready, hid_ready, h_turned, h_copied, \
            y_ready, y_copied = map(sem, ("gcol ycol x_turned x_high x_low up_g up_u silu_ready hid_ready "
                                          "h_turned h_copied y_ready y_copied").split())
        block = c.enter_context(nc.Block())

        def column(t, k):
            return t[:, bass.ds(k, 1)]

        def turns(eng, step, first, end):
            with eng.Fori(first, end) as turn:
                for j in range(J):
                    step(turn * J + j, j)

        def wait(eng, sem_, k, back):
            if not isinstance(k, int) or k - back >= 0:
                eng.wait_ge(sem_, k - back + 1)

        @block.gpsimd
        def _(pool):
            def gather(k, j):
                wait(pool, x_turned, k, J)
                nc.gpsimd.tensor_copy(colG[j][:, :], column(rowG, k)).then_inc(gcol, 1)
                pool.wait_ge(gcol, k + 1)
                pool.sem_inc(passed, 1)
                nc.gpsimd.indirect_dma_start(
                    xg[j][:, :], None, W["xw_dram"], bass.IndirectOffsetOnAxis(ap=colG[j][:, :], axis=0)
                ).then_inc(gathered[j], 16)

            def scatter(k, j):
                wait(pool, y_copied, k, 0)
                nc.gpsimd.tensor_copy(colY[j][:, :], column(rowY, k)).then_inc(ycol, 1)
                pool.wait_ge(ycol, k + 1)
                pool.sem_inc(passed, 1)
                nc.gpsimd.indirect_dma_start(
                    W["y_dram"], bass.IndirectOffsetOnAxis(ap=colY[j][:, :], axis=0), yb[j][:, :], None
                ).then_inc(scattered[j], 16)

            def step(k, j):
                if not isinstance(k, int) or k >= J:
                    scatter(k - J, j)
                gather(k, j)
            for k in range(J):
                step(k, k)
            turns(pool, step, 1, KT // J)
            for k in range(KT - J, KT):
                scatter(k, k % J)
            for j in range(J):
                pool.wait_ge(scattered[j], 16 * (KT // J))

        @block.vector
        def _(dve):
            def rest_x(k, j):
                wait(dve, x_high, k, 0)
                wait(dve, up_u, k, 2)
                nc.vector.tensor_tensor(xTl[j % 2][:, :], psX[:, 0:P], xTh[j % 2][:, :],
                                        ALU.subtract).then_inc(x_low, 1)

            def multiply(k, j):
                wait(dve, silu_ready, k, 0)
                wait(dve, up_u, k, 0)
                wait(dve, h_turned, k, 2)
                nc.vector.tensor_tensor(hid[j % 2][:, :], sg[j % 2][:, :], psU[j % 2][:, :],
                                        ALU.mult).then_inc(hid_ready, 1)

            def take_y(k, j, turn):
                wait(dve, y_ready, k, 0)
                if not isinstance(k, int) or k >= J:
                    dve.wait_ge(scattered[j], turn * 16)
                nc.vector.tensor_copy(yb[j][:, :], psY[j % 2][:, 0:D]).then_inc(y_copied, 1)

            rest_x(0, 0)
            rest_x(1, 1)
            for k in range(2 * J):
                multiply(k, k % J)
                rest_x(k + AHEAD, (k + AHEAD) % J)
                if k >= LAG:
                    take_y(k - LAG, (k - LAG) % J, (k - LAG) // J)
                at = slice(k * XCOLS, (k + 1) * XCOLS)
                nc.vector.scalar_tensor_tensor(X[:, at, :], XN[:, at, :], 0.5, X[:, at, :], ALU.mult, ALU.add)
            with dve.Fori(2, KT // J - 1) as turn:
                for j in range(J):
                    k = turn * J + j
                    multiply(k, j)
                    rest_x(k + AHEAD, (j + AHEAD) % J)
                    take_y(k - LAG, (j - LAG) % J, turn + (j - LAG) // J)
            for k in range(KT - J, KT + LAG):
                if k < KT:
                    multiply(k, k % J)
                if k + AHEAD < KT:
                    rest_x(k + AHEAD, (k + AHEAD) % J)
                take_y(k - LAG, (k - LAG) % J, (k - LAG) // J)

        @block.scalar
        def _(act):
            def copy_x(k, j):
                wait(act, x_turned, k, 0)
                wait(act, up_u, k, 2)
                nc.scalar.activation(xTh[j % 2][:, :], psX[:, 0:P], ACT.Copy).then_inc(x_high, 1)

            def silu(k, j):
                wait(act, up_g, k, 0)
                wait(act, hid_ready, k, 2)
                nc.scalar.activation(sg[j % 2][:, :], psG[j % 2][:, :], ACT.Silu).then_inc(silu_ready, 1)

            def copy_h(k, j):
                wait(act, h_turned, k, 0)
                wait(act, y_ready, k, 2)
                nc.scalar.activation(hT[j % 2][:, :], psH[:, :], ACT.Copy).then_inc(h_copied, 1)

            def step(k, j):
                inside = not isinstance(k, int)
                if inside or k < KT:
                    silu(k, j)
                if inside or k + AHEAD < KT:
                    copy_x(k + AHEAD, j)
                if inside or k >= 1:
                    copy_h(k - 1, j + 1)
            copy_x(0, 0)
            copy_x(1, 1)
            for k in range(J):
                step(k, k % J)
            turns(act, step, 1, KT // J - 1)
            for k in range(KT - J, KT + 1):
                step(k, k)

        @block.tensor
        def _(pe):
            def turn_x(k, j, turn):
                pe.wait_ge(gathered[j], turn * 16 + 16)
                wait(pe, x_low, k, 1)
                nc.tensor.transpose(psX[:, 0:P], xg[j][:, :], W["ident"][:, :]).then_inc(x_turned, 1)

            def expert(k):
                return pe.value_load(expertW[0:1, bass.ds(k, 1)], min_val=0, max_val=E - 1)

            def up(k, j, e):
                wait(pe, x_high, k, 0)
                wait(pe, silu_ready, k, 2)
                wait(pe, hid_ready, k, 2)
                at = bass.ds(e * H, H)
                high, low, g, u = xTh[j % 2][:, :], xTl[j % 2][:, :], psG[j % 2][:, :], psU[j % 2][:, :]
                nc.tensor.matmul(g, high, W["W1h"][:, at], start=True, stop=False)
                nc.tensor.matmul(g, high, W["W1l"][:, at], start=False, stop=False)
                nc.tensor.matmul(u, high, W["W3h"][:, at], start=True, stop=False)
                nc.tensor.matmul(u, high, W["W3l"][:, at], start=False, stop=False)
                wait(pe, x_low, k, 0)
                nc.tensor.matmul(g, low, W["W1h"][:, at], start=False, stop=True).then_inc(up_g, 1)
                nc.tensor.matmul(u, low, W["W3h"][:, at], start=False, stop=True).then_inc(up_u, 1)

            def turn_h(k, j):
                wait(pe, hid_ready, k, 0)
                wait(pe, h_copied, k, 1)
                for q in range(HC):
                    last = nc.tensor.transpose(psH[:, q * P:(q + 1) * P], hid[j % 2][:, q * P:(q + 1) * P],
                                               W["ident"][:, :])
                last.then_inc(h_turned, 1)

            def down(k, j, e):
                wait(pe, h_copied, k, 0)
                wait(pe, y_copied, k, 2)
                for q in range(HC):
                    last = nc.tensor.matmul(psY[j % 2][:, 0:D], hT[j % 2][:, q * P:(q + 1) * P],
                                            W["W2s"][:, bass.ds(e * (HC * D) + q * D, D)],
                                            start=(q == 0), stop=(q == HC - 1))
                last.then_inc(y_ready, 1)

            def steps_of(tiles, turn):
                e = {0: expert(tiles[0][0])}
                for at, (k, j) in enumerate(tiles):
                    inside = not isinstance(k, int)
                    if inside or k < KT:
                        up(k, j, e[at])
                    if inside or k + AHEAD < KT:
                        turn_x(k + AHEAD, (j + AHEAD) % J, turn + (j + AHEAD) // J)
                    if at + 1 < len(tiles) and (inside or k + 1 < KT):
                        e[at + 1] = expert(tiles[at + 1][0])
                    if inside or 1 <= k <= KT:
                        turn_h(k - 1, j + 1)
                    if inside or k >= LAG:
                        down(k - LAG, j, e[at - LAG] if at >= LAG else expert(k - LAG))

            if layer == 0:
                pe.wait_ge(W["w2_came"], 16)
            turn_x(0, 0, 0)
            turn_x(1, 1, 0)
            steps_of([(k, k) for k in range(J)], 0)
            with pe.Fori(1, KT // J - 1) as turn:
                steps_of([(turn * J + j, j) for j in range(J)], turn)
            steps_of([(k, k - (KT - J)) for k in range(KT - J, KT + LAG)], KT // J - 1)


def combine(nc, W):
    X = W["X"]
    with ExitStack() as c:
        ya = c.enter_context(nc.sbuf_tensor("ya", [P, S, NT, D], F32))
        sem = lambda n: c.enter_context(nc.semaphore(n))
        sent = sem("sent")
        block = c.enter_context(nc.Block())
        W["summed_from"] = W["own_steps"]

        @block.vector
        def _(dve):
            link = linker(dve, W)
            for b in range(SEQS):
                add_outputs(nc, dve, link, W, ya, 1, b)

        @block.sync
        def _(sp):
            load_outputs(sp, W, ya)
            res = W["out"].rearrange("b (i p) d -> p (b i) d", p=P)
            for b in range(SEQS):
                at = slice(TS * b, TS * (b + 1))
                sp.wait_ge(W["own_step"], W["summed_from"] + 2 * (b + 1))
                sp.dma_start(res[:, at, :], X[:, at, :]).then_inc(sent, 16)
            sp.wait_ge(sent, 16 * SEQS)


def steps(nc, W):
    XT, DT, BC3 = W["XT"], W["DT"], W["BC3"]
    C = 2 * N
    RB = 4
    with ExitStack() as c:
        tb = lambda n, shape: c.enter_context(nc.sbuf_tensor(n, shape, F32))
        ps = lambda n: c.enter_context(nc.psum_tensor(n, [P, BANK], F32))
        sem = lambda n: c.enter_context(nc.semaphore(n))
        W_in3 = tb("W_in3", [D, 3, C])
        b_in3 = tb("b_in3", [3 * C, 1])
        rT = [tb(f"rT{j}", [R, BANK]) for j in range(2)]
        bc = [tb(f"bc{j}", [3 * C, BANK]) for j in range(RB)]
        u = W["XN"][:, :, :].rearrange("p i d -> p (i d)")
        lost = tb("lost", [D, T])
        psr = [ps(f"psr{j}") for j in range(2)]
        psz = [ps(f"psz{j}") for j in range(2)]
        psbc = [ps(f"psbc{j}") for j in range(2)]
        b3_loaded, w3_ready, low, low_c, bc_done, bc_taken, z_done, abs_ready, relu_ready, u_ready, ln_ready, \
            lead_ready, rest_ready, mid_ready, last_ready, g_ready, lost_ready, base_ready, added = map(
                sem, ("b3_loaded w3_ready low low_c bc_done bc_taken z_done abs_ready relu_ready u_ready ln_ready "
                      "lead_ready rest_ready mid_ready last_ready g_ready lost_ready base_ready added").split())
        block = c.enter_context(nc.Block())
        cut = lambda t, q: t[:, q * BANK:(q + 1) * BANK]

        @block.sync
        def _(sp):
            for g in range(3):
                sp.dma_start(b_in3[g * C:(g + 1) * C, :],
                             W["b_in"].rearrange("(c a) -> c a", a=1)).then_inc(b3_loaded, 16)

        @block.tensor
        def _(pe):
            for q in range(QN + 1):
                if q < QN:
                    if q >= 2:
                        pe.wait_ge(low_c, q - 1)
                    nc.tensor.matmul(psr[q % 2][0:R, :], W["W_dt1s"][:, :], cut(XT, q), start=True,
                                     stop=True).then_inc(low, 1)
                    if q == 0:
                        pe.wait_ge(w3_ready, 1)
                    if q >= 2:
                        pe.wait_ge(bc_taken, q - 1)
                    nc.tensor.matmul(psbc[q % 2][0:3 * C, :], W_in3[:, :, :].rearrange("d g c -> d (g c)"),
                                     cut(XT, q), start=True, stop=True).then_inc(bc_done, 1)
                if q >= 1:
                    z = q - 1
                    pe.wait_ge(low_c, z + 1)
                    if z >= 2:
                        pe.wait_ge(relu_ready, z - 1)
                    nc.tensor.matmul(psz[z % 2][:, :], W["W_dt2s"][:, :], rT[z % 2][:, :],
                                     start=True, stop=True).then_inc(z_done, 1)

        @block.scalar
        def _(act):
            act.wait_ge(b3_loaded, 48)
            for q in range(QN + 1):
                z = q - 1
                if q < QN:
                    act.wait_ge(low, q + 1)
                    if q >= 2:
                        act.wait_ge(z_done, q - 1)
                    nc.scalar.activation(rT[q % 2][:, :], psr[q % 2][0:R, :], ACT.Identity,
                                         bias=W["b_dt1c"][:, :]).then_inc(low_c, 1)
                if q >= 1:
                    act.wait_ge(z_done, z + 1)
                    nc.scalar.activation(cut(u, z), psz[z % 2][:, :], ACT.Abs,
                                         bias=W["b_dt2c"][:, :]).then_inc(abs_ready, 1)
                if q < QN:
                    act.wait_ge(bc_done, q + 1)
                    if q >= RB:
                        act.wait_ge(last_ready, q - RB + 1)
                    nc.scalar.activation(bc[q % RB][:, :], psbc[q % 2][0:3 * C, :], ACT.Identity,
                                         bias=b_in3[:, :]).then_inc(bc_taken, 1)
                if q >= 1:
                    act.wait_ge(abs_ready, z + 1)
                    nc.scalar.activation(cut(u, z), cut(u, z), ACT.Exp, scale=-1.0).then_inc(u_ready, 1)
            for q in range(QN):
                act.wait_ge(lost_ready, q + 1)
                nc.scalar.activation(cut(u, q), cut(u, q), ACT.Ln, bias=1.0).then_inc(ln_ready, 1)

        @block.gpsimd
        def _(pool):
            for q in range(QN + 3):
                if q < QN:
                    pool.wait_ge(lead_ready, q + 1)
                    b = bc[q % RB]
                    nc.gpsimd.tensor_tensor(b[0:2 * C, :], b[0:2 * C, :], cut(BC3, q)[0:2 * C, :],
                                            ALU.subtract).then_inc(rest_ready, 1)
                if 1 <= q <= QN:
                    pool.wait_ge(mid_ready, q)
                    b, last = bc[(q - 1) % RB], cut(BC3, q - 1)[0:C, :]
                    nc.gpsimd.tensor_tensor(last, b[0:C, :], last, ALU.subtract).then_inc(last_ready, 1)
                if q >= 3:
                    z = q - 3
                    pool.wait_ge(g_ready, z + 1)
                    nc.gpsimd.tensor_tensor(cut(lost, z), cut(u, z), cut(lost, z), ALU.subtract).then_inc(lost_ready, 1)

        @block.vector
        def _(dve):
            v = nc.vector
            v.tensor_scalar(W["Ahalf"][:, :], W["As"][:, :], 0.5, None, ALU.mult)
            v.reciprocal(W["Ainv"][:, :], W["As"][:, :])
            v.tensor_copy(W_in3[:, :, :], W["W_ins"][:, :].unsqueeze(1).to_broadcast([D, 3, C])).then_inc(w3_ready, 1)
            for q in range(QN + 4):
                if q < QN:
                    dve.wait_ge(bc_taken, q + 1)
                    v.tensor_copy(cut(BC3, q)[0:3 * C, :], bc[q % RB][:, :]).then_inc(lead_ready, 1)
                if 1 <= q <= QN:
                    z = q - 1
                    dve.wait_ge(abs_ready, z + 1)
                    v.tensor_scalar(cut(DT, z), psz[z % 2][:, :], W["b_dt2c"][:, :], 0.0, ALU.add,
                                    ALU.max).then_inc(relu_ready, 1)
                    dve.wait_ge(rest_ready, q)
                    v.tensor_copy(cut(BC3, z)[0:2 * C, :], bc[z % RB][0:2 * C, :]).then_inc(mid_ready, 1)
                if 2 <= q <= QN + 1:
                    z = q - 2
                    dve.wait_ge(u_ready, z + 1)
                    v.tensor_scalar(cut(lost, z), cut(u, z), 1.0, -1.0, ALU.add, ALU.add).then_inc(g_ready, 1)
                if q >= 4:
                    z = q - 4
                    dve.wait_ge(lost_ready, z + 1)
                    v.tensor_tensor(cut(DT, z), cut(DT, z), cut(lost, z), ALU.add).then_inc(base_ready, 1)
            for q in range(QN + 1):
                if q < QN:
                    dve.wait_ge(base_ready, q + 1)
                    dve.wait_ge(ln_ready, q + 1)
                    v.tensor_tensor(cut(DT, q), cut(DT, q), cut(u, q), ALU.add).then_inc(added, 1)
                if q >= 1:
                    dve.wait_ge(added, q)
                    v.tensor_scalar(cut(DT, q - 1), cut(DT, q - 1), DT_MIN, DT_MAX, ALU.max, ALU.min)


def scan(nc, W):
    XT, DT, BC3 = W["XT"], W["DT"], W["BC3"]
    UN = T // BANK
    RING = 4
    PIECES = L // BANK
    BX_DVE = range(3, N, 4)
    BX_POOL = [n for n in range(N) if n not in BX_DVE]
    with ExitStack() as c:
        tb = lambda n, shape, dt=F32: c.enter_context(nc.sbuf_tensor(n, shape, dt))
        ps = lambda n: c.enter_context(nc.psum_tensor(n, [P, BANK], F32))
        sem = lambda n: c.enter_context(nc.semaphore(n))
        pick = W["pick"]
        th = [tb(f"th{j}", [D, BANK]) for j in range(RING)]
        bsb = [tb(f"bsb{j}", [D, BANK]) for j in range(2)]
        bxs = [tb(f"bxs{j}", [D, BANK]) for j in range(RING)]
        drv = [tb(f"drv{j}", [D, BANK]) for j in range(2)]
        h = [tb(f"h{j}", [D, BANK]) for j in range(2)]
        hc = [tb(f"hc{j}", [D, BANK]) for j in range(RING)]
        start = tb("start", [D, PIECES, N])
        abar = [ps(f"abar{j}") for j in range(RING)]
        psB, psY = ps("psBs"), ps("psYs")
        psC = [ps(f"psCs{j}") for j in range(2)]
        start_clear, b_there, b_kept, c_there, c_used, decayed, halved, h_kept, driven, bx_pool, bx_dve, expm1_there, \
            recurred, c_summed, y_taken, passed = map(
                sem, ("start_clear b_there b_kept c_there c_used decayed halved h_kept driven bx_pool "
                      "bx_dve expm1_there recurred c_summed y_taken passed").split())
        block = c.enter_context(nc.Block())

        def walk(*ops):
            def piece(u):
                for n in range(N):
                    for lead, op in ops:
                        du, dn = divmod(n + lead, N)
                        if not isinstance(u, int) or 0 <= u + du < UN:
                            op(u + du, dn)
            return piece

        def run(eng, *ops):
            piece = walk(*ops)
            for lead in range(5, 0, -1):
                for its, op in ops:
                    if its >= lead:
                        op(0, its - lead)
            piece(0)
            with eng.Fori(1, UN - 1) as u:
                piece(u)
            piece(UN - 1)
            for n in range(4):
                for lead, op in ops:
                    if n + lead < 0:
                        op(UN - 1, N + n + lead)

        def wait(eng, sem_, u, n, back=0, states=range(N)):
            du, dn = divmod(n - back, N)
            more = du * len(states) + len([k for k in states if k <= dn])
            if not isinstance(u, int) or u * len(states) + more > 0:
                eng.wait_ge(sem_, u * len(states) + more)

        def wait_bx(eng, u, n):
            if n in BX_DVE:
                wait(eng, bx_dve, u, n, 0, BX_DVE)
            else:
                wait(eng, bx_pool, u, n, 0, BX_POOL)

        def later(u):
            return not isinstance(u, int) or u > 0

        def cols(t, u):
            return t[:, bass.ds(u * BANK, BANK)]

        @block.tensor
        def _(pe):
            def spread_b(u, n):
                if (n - 1) % N in BX_DVE:
                    wait(pe, bx_dve, u, n, 1, BX_DVE)
                else:
                    wait(pe, b_kept, u, n, 1, BX_POOL)
                nc.tensor.matmul(psB[:, :], pick[:, n, :], cols(BC3, u), start=True, stop=True).then_inc(b_there, 1)

            def spread_c(u, n):
                wait(pe, c_used, u, n, 2)
                nc.tensor.matmul(psC[n % 2][:, :], pick[:, N + n, :], cols(BC3, u), start=True,
                                 stop=True).then_inc(c_there, 1)

            def sum_c(u, n):
                wait(pe, c_used, u, n)
                if n == 0 and later(u):
                    pe.wait_ge(y_taken, u)
                nc.tensor.matmul(psY[:, :], W["ident"][:, :], hc[n % RING][:, :], start=(n == 0),
                                 stop=(n == N - 1)).then_inc(c_summed, 1)

            run(pe, (5, spread_b), (-2, sum_c), (1, spread_c))

        @block.scalar
        def _(act):
            def keep_h(u, n):
                wait(act, recurred, u, n)
                nc.scalar.activation(start[:, 1, n:n + 1], h[n % 2][:, BANK - 1:BANK], ACT.Copy).then_inc(h_kept, 1)

            def decay(u, n):
                wait(act, recurred, u, n, RING)
                wait(act, driven, u, n, RING)
                act.sem_inc(passed, 1)
                nc.scalar.activation(abar[n % RING][:, :], cols(DT, u), ACT.Exp,
                                     scale=W["As"][:, n:n + 1]).then_inc(decayed, 1)
                nc.scalar.activation(th[n % RING][:, :], cols(DT, u), ACT.Tanh,
                                     scale=W["Ahalf"][:, n:n + 1]).then_inc(halved, 1)

            def keep_b(u, n):
                if n not in BX_POOL:
                    return
                wait(act, b_there, u, n)
                wait(act, bx_pool, u, n, 2, BX_POOL)
                nc.scalar.activation(bsb[n % 2][:, :], psB[:, :], ACT.Copy).then_inc(b_kept, 1)

            run(act, (-1, keep_h), (3, decay), (4, keep_b))

        @block.gpsimd
        def _(pool):
            def drive(u, n):
                wait(pool, expm1_there, u, n)
                wait_bx(pool, u, n)
                wait(pool, recurred, u, n, 2)
                nc.gpsimd.tensor_tensor(drv[n % 2][:, :], th[n % RING][:, :], bxs[n % RING][:, :],
                                        ALU.mult).then_inc(driven, 1)

            def bx(u, n):
                if n not in BX_POOL:
                    return
                wait(pool, b_kept, u, n, 0, BX_POOL)
                wait(pool, driven, u, n, RING)
                pool.sem_inc(passed, 1)
                nc.gpsimd.tensor_tensor(bxs[n % RING][:, :], bsb[n % 2][:, :], cols(XT, u),
                                        ALU.mult).then_inc(bx_pool, 1)

            run(pool, (1, drive), (3, bx))

        @block.vector
        def _(dve):
            v = nc.vector

            def expm1(u, n):
                wait(dve, decayed, u, n)
                wait(dve, halved, u, n)
                v.scalar_tensor_tensor(th[n % RING][:, :], abar[n % RING][:, :], 1.0, th[n % RING][:, :], ALU.add,
                                       ALU.mult).then_inc(expm1_there, 1)

            def bx(u, n):
                if n not in BX_DVE:
                    return
                wait(dve, b_there, u, n)
                wait(dve, driven, u, n, RING)
                v.tensor_tensor(bxs[n % RING][:, :], psB[:, :], cols(XT, u), ALU.mult).then_inc(bx_dve, 1)

            def recur(u, n):
                wait(dve, driven, u, n)
                wait(dve, c_used, u, n, 2)
                wait(dve, h_kept, u, n, 2)
                v.tensor_tensor_scan(h[n % 2][:, :], abar[n % RING][:, :], drv[n % 2][:, :],
                                     starts(u, n), ALU.mult, ALU.add).then_inc(recurred, 1)

            def starts(u, n):
                if isinstance(u, int):
                    return start[:, u % PIECES, n:n + 1]
                return start[:, bass.ds(u % PIECES, 1), n:n + 1].rearrange("d a n -> d (a n)")

            def times_c(u, n):
                wait(dve, recurred, u, n)
                wait(dve, c_there, u, n)
                wait(dve, c_summed, u, n, RING)
                v.scalar_tensor_tensor(hc[n % RING][:, :], h[n % 2][:, :], W["Ainv"][:, n:n + 1], psC[n % 2][:, :],
                                       ALU.mult, ALU.mult).then_inc(c_used, 1)

            def take_y(u, n):
                if n == N - 1:
                    wait(dve, c_summed, u, n)
                    v.scalar_tensor_tensor(cols(XT, u), cols(XT, u), W["Dc"][:, :], psY[:, :], ALU.mult,
                                           ALU.add).then_inc(y_taken, 1)

            v.memset(start[:, :, :], 0.0).then_inc(start_clear, 1)
            dve.wait_ge(start_clear, 1)
            run(dve, (4, bx), (2, expm1), (0, recur), (-1, times_c), (-3, take_y))


_INS = ['L0_attn_x', 'L0_attn_W_in', 'L0_attn_b_in', 'L0_attn_W_dt1', 'L0_attn_b_dt1', 'L0_attn_W_dt2',
        'L0_attn_b_dt2', 'L0_attn_A', 'L0_attn_D', 'L0_ffn_Wg', 'L0_ffn_bg', 'L0_ffn_W1', 'L0_ffn_W2', 'L0_ffn_W3']


def kernel(**inputs):
    import numpy as np
    import concourse.bacc as bacc
    from concourse.bass_utils import run_bass_kernel_spmd

    nc = bacc.Bacc("TRN2", target_bir_lowering=False, num_devices=1)
    arrays, args = {}, []
    for name in _INS:
        a = np.ascontiguousarray(inputs[name])
        arrays[f"in_{name}"] = a
        args.append(nc.dram_tensor(f"in_{name}", a.shape, mybir.dt.from_np(a.dtype), kind="ExternalInput").ap())
    shape = inputs['L0_attn_x'].shape
    out = nc.dram_tensor("out_x", shape, F32, kind="ExternalOutput").ap()
    macaron(nc, *args, out)
    r = run_bass_kernel_spmd(nc, [arrays], core_ids=[0])
    return r.results[0]["out_x"]
```

```python
import concourse.bass as bass
from concourse import mybir
from contextlib import ExitStack

F32 = mybir.dt.float32
I32 = mybir.dt.int32
BF16 = mybir.dt.bfloat16
F32R = mybir.dt.float32r
ALU = mybir.AluOpType
ACT = mybir.ActivationFunctionType
AX = mybir.AxisListType

P = 128
D = 128
SEQS, L = 4, 1024
T = SEQS * L
NT = T // P
TS = L // P
N = 16
R = 64
E, H = 8, 512
HC = H // P
S = 2
KT = S * T // P + E
BANK = 512
QN = T // BANK
EPS = 1e-5
BIG = 3.0e38
SMALL = 10
DT_MIN, DT_MAX = 1e-7, 1e6


def linker(dve, W):
    def link(ins):
        W["own_steps"] += 1
        ins.then_inc(W["own_step"], 1)
        dve.wait_ge(W["own_step"], W["own_steps"])
    return link


def macaron(nc, x, W_in, b_in, W_dt1, b_dt1, W_dt2, b_dt2, A, Dp, Wg, bg, W1, W2, W3, out):
    xw_dram = nc.dram_tensor("xw_dram", (S * T, D), F32).ap()
    y_dram = nc.dram_tensor("y_dram", (S * T + KT * P, D), F32).ap()

    with ExitStack() as whole:
        def sb(name, shape, dt=F32):
            return whole.enter_context(nc.sbuf_tensor(name, shape, dt))

        X = sb("X", [P, NT, D])
        XN = sb("XN", [P, NT, D])
        XT = sb("XT", [D, T])
        W1h, W1l = sb("W1h", [D, E * H], F32R), sb("W1l", [D, E * H], F32R)
        W3h, W3l = sb("W3h", [D, E * H], F32R), sb("W3l", [D, E * H], F32R)
        W2s = sb("W2s", [P, E * HC * D])
        ident = sb("ident", [P, P])
        ones = sb("ones", [P, P])
        before = sb("before", [P, P])
        Wgs = sb("Wgs", [D, E])
        bgB = sb("bgB", [P, E])
        W_ins = sb("W_ins", [D, 2 * N])
        b_inc = sb("b_inc", [2 * N, 1])
        pick = sb("pick", [3 * 2 * N, 2 * N, P], BF16)
        W_dt1s = sb("W_dt1s", [D, R])
        b_dt1c = sb("b_dt1c", [R, 1])
        W_dt2s = sb("W_dt2s", [R, D])
        b_dt2c = sb("b_dt2c", [D, 1])
        As = sb("As", [D, N])
        Dc = sb("Dc", [D, 1])
        Ahalf = sb("Ahalf", [D, N])
        Ainv = sb("Ainv", [D, N])
        first = sb("first", [P, S, NT])
        rowno = sb("rowno", [P, 1])
        rev = sb("rev", [P, E])
        iotaR = sb("iotaR", [P, P])
        iotaK = sb("iotaK", [P, KT])
        padrow = sb("padrow", [P, KT])
        notfirst = sb("notfirst", [P, E, NT])
        came = [whole.enter_context(nc.semaphore(f"came{b}")) for b in range(SEQS)]
        bc_packed = [whole.enter_context(nc.semaphore(f"bc_packed{j}")) for j in range(3)]
        gathered = [whole.enter_context(nc.semaphore(f"gathered{j}")) for j in range(8)]
        scattered = [whole.enter_context(nc.semaphore(f"scattered{j}")) for j in range(8)]
        passed = whole.enter_context(nc.semaphore("passed"))
        small_came = whole.enter_context(nc.semaphore("small_came"))
        w13_came = [whole.enter_context(nc.semaphore(f"w{m}_came")) for m in (1, 3)]
        w2_came = whole.enter_context(nc.semaphore("w2_came"))
        pick_made = whole.enter_context(nc.semaphore("pick_made"))
        own_step = whole.enter_context(nc.semaphore("own_step"))
        own_steps = 0
        W = dict(locals())

        for layer in range(2):
            with ExitStack() as ffn:
                def tb(name, shape, dt=F32):
                    return ffn.enter_context(nc.sbuf_tensor(f"{name}_{layer}", shape, dt))
                W["rowG"] = tb("rowG", [P, KT], I32)
                W["rowY"] = tb("rowY", [P, KT], I32)
                W["expertW"] = tb("expertW", [P, KT], I32)
                with nc.psum_tensor(f"psL_{layer}", [P, BANK], F32) as psL:
                    W["psL"] = psL
                    if layer == 0:
                        with nc.sbuf_tensor("W1raw", [D, E * H], F32) as W1raw, \
                                nc.sbuf_tensor("W3raw", [D, E * H], F32) as W3raw:
                            W["W1raw"], W["W3raw"] = W1raw, W3raw
                            load_and_constants(nc, W)
                            normalise(nc, W, "n0", loads=True, combines=False, scanned=False, gate=True)
                    else:
                        normalise(nc, W, "n1", loads=False, combines=False, scanned=True, gate=True)
                    route(nc, W, layer)
                experts(nc, W, layer)
            if layer == 0:
                normalise(nc, W, "nm", loads=False, combines=True, scanned=False, gate=False)
                with nc.sbuf_tensor("DT", [D, T], F32) as DT, nc.sbuf_tensor("Btok", [P, NT, N], F32) as Btok, \
                        nc.sbuf_tensor("BC3", [3 * 2 * N, T], BF16) as BC3:
                    W["DT"], W["Btok"], W["BC3"] = DT, Btok, BC3
                    steps(nc, W)
                    scan(nc, W)
        combine(nc, W)


def load_weights(sp, W):
    small = [(W["Wgs"], W["Wg"]), (W["bgB"], W["bg"].partition_broadcast(P)),
             (W["W_ins"], W["W_in"]),
             (W["b_inc"], W["b_in"].rearrange("(r a) -> r a", a=1)),
             (W["W_dt1s"], W["W_dt1"]), (W["W_dt2s"], W["W_dt2"]),
             (W["b_dt1c"], W["b_dt1"].rearrange("(r a) -> r a", a=1)),
             (W["b_dt2c"], W["b_dt2"].rearrange("(r a) -> r a", a=1)),
             (W["As"], W["A"].rearrange("a b d n -> (a b d) n")),
             (W["Dc"], W["Dp"].rearrange("(r a) -> r a", a=1))]
    assert len(small) == SMALL
    for dst, src in small:
        sp.dma_start(dst[:, :], src).then_inc(W["small_came"], 16)
    for raw, src, came in ((W["W1raw"], W["W1"], W["w13_came"][0]), (W["W3raw"], W["W3"], W["w13_came"][1])):
        sp.dma_start(raw[:, :].rearrange("d (e h) -> d e h", e=E),
                     src.rearrange("e d h -> d e h")).then_inc(came, 16)
    sp.dma_start(W["W2s"][:, :].rearrange("p (e c d) -> p e c d", e=E, c=HC),
                 W["W2"].rearrange("e (c p) d -> p e c d", p=P)).then_inc(W["w2_came"], 16)


def load_and_constants(nc, W):
    with ExitStack() as c:
        made = c.enter_context(nc.semaphore("made"))
        block = c.enter_context(nc.Block())

        @block.sync
        def _(sp):
            for b in range(SEQS):
                sp.dma_start(W["X"][:, b * TS:(b + 1) * TS, :],
                             W["x"][b].rearrange("(i p) d -> p i d", p=P)).then_inc(W["came"][b], 16)

        @block.gpsimd
        def _(pool):
            nc.gpsimd.memset(W["ident"][:, :], 0.0).then_inc(made, 1)
            nc.gpsimd.memset(W["before"][:, :], 1.0).then_inc(made, 1)
            nc.gpsimd.memset(W["ones"][:, :], 1.0)
            pool.wait_ge(made, 2)
            nc.gpsimd.affine_select(out=W["ident"][:, :], in_=W["ident"][:, :], compare_op=ALU.not_equal,
                                    fill=1.0, base=0, pattern=[[-1, P]], channel_multiplier=1)
            nc.gpsimd.affine_select(out=W["before"][:, :], in_=W["before"][:, :], compare_op=ALU.is_gt,
                                    fill=0.0, base=0, pattern=[[1, P]], channel_multiplier=-1)
            nc.gpsimd.iota(W["first"][:, :, :], pattern=[[T, S], [P, NT]], base=0, channel_multiplier=0,
                           allow_small_or_imprecise_dtypes=True)
            nc.gpsimd.iota(W["rowno"][:, :], pattern=[[0, 1]], base=1, channel_multiplier=1,
                           allow_small_or_imprecise_dtypes=True)
            nc.gpsimd.iota(W["rev"][:, :], pattern=[[-1, E]], base=E, channel_multiplier=0,
                           allow_small_or_imprecise_dtypes=True)
            nc.gpsimd.iota(W["iotaR"][:, :], pattern=[[1, P]], base=0, channel_multiplier=0,
                           allow_small_or_imprecise_dtypes=True)
            nc.gpsimd.iota(W["iotaK"][:, :], pattern=[[1, KT]], base=0, channel_multiplier=0,
                           allow_small_or_imprecise_dtypes=True)
            nc.gpsimd.iota(W["padrow"][:, :], pattern=[[P, KT]], base=S * T + 1, channel_multiplier=1,
                           allow_small_or_imprecise_dtypes=True)

        @block.vector
        def _(dve):
            link = linker(dve, W)
            link(nc.vector.memset(W["notfirst"][:, :, :], 1.0))
            nc.vector.memset(W["notfirst"][:, :, 0:1], 0.0)


def normalise(nc, W, tag, loads, combines, scanned, gate):
    per = BANK // P
    X, XN, XT, ident = W["X"], W["XN"], W["XT"], W["ident"]
    with ExitStack() as c:
        tb = lambda n, shape: c.enter_context(nc.sbuf_tensor(f"{n}_{tag}", shape, F32))
        sq = tb("sq", [P, NT, D])
        less = tb("less", [P, NT])
        ssq = tb("ssq", [P, NT])
        rstd = tb("rstd", [P, NT])
        unit = tb("unit", [P, 1])
        ya = tb("ya", [P, S, NT, D]) if combines else None
        psT = [c.enter_context(nc.psum_tensor(f"psT{j}_{tag}", [P, BANK], F32)) for j in range(4)]
        sem = lambda n: c.enter_context(nc.semaphore(f"{n}_{tag}"))
        shared = 0 if loads else 1
        xn_pool, rstd_ready = (sem("xn_pool"), sem("rstd_ready")) if shared else (None, None)
        unit_ready, meaned, squared, var_ready, sd_ready, xn_ready, turned, copied = map(
            sem, "unit_ready meaned squared var_ready sd_ready xn_ready turned copied".split())
        adds = combines or scanned
        psV = [c.enter_context(nc.psum_tensor(f"psV{j}_{tag}", [P, BANK], F32)) for j in range(3)] if adds else None
        brought, added = (sem("brought"), sem("added")) if adds else (None, None)
        block = c.enter_context(nc.Block())

        parts = [(W["W1raw"], W["W1h"], W["W1l"]), (W["W3raw"], W["W3h"], W["W3l"])] if loads else []
        high_made = sem("high_made") if loads else None
        LATE = 4

        def part(k):
            raw, high, low = parts[k // E]
            at = slice(k % E * H, (k % E + 1) * H)
            return low[:, at], raw[:, at], high[:, at]

        def seq(t, b):
            return t[:, TS * b:TS * (b + 1), :]

        if loads:
            @block.sync
            def _(sp):
                load_weights(sp, W)

        if combines:
            @block.sync
            def _(sp):
                load_outputs(sp, W, ya)

        @block.gpsimd
        def _(pool):
            if loads:
                for k in range(2 * E - LATE):
                    pool.wait_ge(high_made, k + 1)
                    nc.gpsimd.tensor_tensor(*part(k), ALU.subtract)
            if shared:
                for q in range(QN):
                    i = q * per
                    pool.wait_ge(rstd_ready, q // 2 + 1)
                    nc.gpsimd.tensor_scalar(XN[:, i, :], X[:, i, :], less[:, i:i + 1], rstd[:, i:i + 1], ALU.add,
                                            ALU.mult).then_inc(xn_pool, 1)

        @block.vector
        def _(dve):
            link = linker(dve, W)
            v = nc.vector
            v.memset(unit[:, :], 1.0).then_inc(unit_ready, 1)
            for b in range(SEQS + 1):
                if b < SEQS:
                    cols = slice(TS * b, TS * (b + 1))
                    if loads:
                        dve.wait_ge(W["came"][b], 16)
                    if adds:
                        for q in (2 * b, 2 * b + 1):
                            at = X[:, q * per:(q + 1) * per, :]
                            more = psV[q % 3][:, :].rearrange("p (i d) -> p i d", d=D)
                            dve.wait_ge(brought, q + 1)
                            v.scalar_tensor_tensor(at, more, 0.5 if combines else 1.0, at, ALU.mult,
                                                   ALU.add).then_inc(added, 1)
                        dve.wait_ge(added, 2 * b + 2)
                    link(v.reduce_sum(less[:, cols], seq(X, b), axis=AX.X))
                    v.tensor_scalar(less[:, cols], less[:, cols], -1.0 / D, None, ALU.mult).then_inc(meaned, 1)
                if b >= 1:
                    cols = slice(TS * (b - 1), TS * b)
                    dve.wait_ge(squared, NT // SEQS * b)
                    v.tensor_scalar(rstd[:, cols], ssq[:, cols], 1.0 / D, EPS, ALU.mult, ALU.add).then_inc(var_ready, 1)
                    dve.wait_ge(sd_ready, b)
                    link(v.reciprocal(rstd[:, cols], rstd[:, cols]))
                    if shared:
                        v.sem_inc(rstd_ready, 1)
                    for i in [i for i in range(TS * (b - 1), TS * b) if i % per >= shared]:
                        v.tensor_scalar(XN[:, i, :], X[:, i, :], less[:, i:i + 1], rstd[:, i:i + 1], ALU.add,
                                        ALU.mult).then_inc(xn_ready, 1)
            if loads:
                for k in range(2 * E - LATE, 2 * E):
                    dve.wait_ge(high_made, k + 1)
                    v.tensor_tensor(*part(k), ALU.subtract)

        @block.scalar
        def _(act):
            def copy_turned(q):
                act.wait_ge(turned, q + 1)
                nc.scalar.activation(XT[:, q * BANK:(q + 1) * BANK], psT[q % 4][:, :],
                                     ACT.Copy).then_inc(copied, 1)

            def take_high(first):
                for k in range(first, first + 4):
                    act.wait_ge(W["w13_came"][k // E], 16)
                    _low, raw, high = part(k)
                    nc.scalar.activation(high, raw, ACT.Copy).then_inc(high_made, 1)

            act.wait_ge(unit_ready, 1)
            nc.scalar.activation(unit[:, :], unit[:, :], ACT.Sqrt)
            for b in range(SEQS + 1):
                if b >= 1:
                    cols = slice(TS * (b - 1), TS * b)
                    act.wait_ge(var_ready, b)
                    nc.scalar.activation(rstd[:, cols], rstd[:, cols], ACT.Sqrt).then_inc(sd_ready, 1)
                if b < SEQS:
                    act.wait_ge(meaned, b + 1)
                    for i in range(TS * b, TS * (b + 1)):
                        nc.scalar.activation(sq[:, i, :], X[:, i, :], ACT.Square, bias=less[:, i:i + 1],
                                             accum_out=ssq[:, i:i + 1]).then_inc(squared, 1)
                if loads and b >= 2:
                    take_high(4 * (b - 2))
                if b >= 1:
                    copy_turned(2 * (b - 1))
                    copy_turned(2 * (b - 1) + 1)
            if loads:
                take_high(2 * E - 4)

        @block.tensor
        def _(pe):
            def bring(q):
                if q >= 3:
                    pe.wait_ge(added, q - 2)
                if combines:
                    pe.wait_ge(W["came"][q // 2], 16 + 16 * S)
                    for s in range(S):
                        last = nc.tensor.matmul(psV[q % 3][:, :], ident[:, :],
                                                ya[:, s, q * per:(q + 1) * per, :].rearrange("p i d -> p (i d)"),
                                                start=(s == 0), stop=(s == S - 1))
                else:
                    for i in range(q * per, (q + 1) * per):
                        last = nc.tensor.transpose(psV[q % 3][:, i % per * P:(i % per + 1) * P],
                                                   XT[:, i * P:(i + 1) * P], ident[:, :])
                last.then_inc(brought, 1)

            def gates(q):
                pe.wait_ge(copied, q + 1)
                for i in range(q * per, (q + 1) * per):
                    nc.tensor.matmul(W["psL"][:, i * E:(i + 1) * E], XT[:, i * P:(i + 1) * P], W["Wgs"][:, :],
                                     start=True, stop=True)

            if loads:
                pe.wait_ge(W["small_came"], 16 * SMALL)
            AHEAD = 6
            if adds:
                for q in range(AHEAD):
                    bring(q)
            for b in range(SEQS):
                if gate and b >= 1:
                    gates(2 * b - 2)
                    gates(2 * b - 1)
                for q in (2 * b, 2 * b + 1):
                    pe.wait_ge(xn_ready, (per - shared) * (q + 1))
                    if shared:
                        pe.wait_ge(xn_pool, q + 1)
                    if q >= 4:
                        pe.wait_ge(copied, q - 3)
                    for j in range(per):
                        last = nc.tensor.transpose(psT[q % 4][:, j * P:(j + 1) * P], XN[:, q * per + j, :],
                                                   ident[:, :])
                    last.then_inc(turned, 1)
                if adds:
                    for q in range(AHEAD + 2 * b, min(AHEAD + 2 * b + 2, QN)):
                        bring(q)
            if gate:
                gates(QN - 2)
                gates(QN - 1)


def load_outputs(sp, W, ya):
    rows = W["y_dram"][0:S * T, :].rearrange("(s i p) d -> p s i d", s=S, p=P)
    for b in range(SEQS):
        for s in range(S):
            at = slice(TS * b, TS * (b + 1))
            sp.dma_start(ya[:, s, at, :], rows[:, s, at, :]).then_inc(W["came"][b], 16)


def add_outputs(nc, dve, link, W, ya, b):
    at = slice(TS * b, TS * (b + 1))
    X = W["X"]
    dve.wait_ge(W["came"][b], 16 + 16 * S * 2)
    link(nc.vector.tensor_tensor(ya[:, 0, at, :], ya[:, 0, at, :], ya[:, 1, at, :], ALU.add))
    link(nc.vector.scalar_tensor_tensor(X[:, at, :], ya[:, 0, at, :], 0.5, X[:, at, :], ALU.mult, ALU.add))


def route(nc, W, layer):
    XN, first, rev, psL = W["XN"], W["first"], W["rev"], W["psL"]
    CH = 8
    NCH = S * NT // CH
    with ExitStack() as c:
        tb = lambda n, shape, dt=F32: c.enter_context(nc.sbuf_tensor(f"{n}_{layer}", shape, dt))
        lg = tb("lg", [P, NT, E])
        tmp = tb("tmp", [P, NT, E])
        oh = [tb(f"oh{s}", [P, NT, E]) for s in range(S)]
        m = [tb(f"m{s}", [P, NT]) for s in range(S)]
        mq = tb("mq", [P, NT])
        chosen = tb("chosen", [P, E, NT])
        tot = tb("tot", [P, E, NT])
        inc = tb("inc", [P, E, NT])
        pos = tb("pos", [P, E, NT])
        cnt = tb("cnt", [P, E], I32)
        tiles = tb("tiles", [P, E])
        tend = tb("tend", [P, E])
        toff = tb("toff", [P, E])
        w = tb("w", [P, S, NT])
        ppos = tb("ppos", [P, S, NT])
        pint = tb("pint", [P, S, NT], I32)
        pk = tb("pk", [P, S, NT])
        pr = tb("pr", [P, S, NT])
        past = tb("past", [P, KT, E])
        nexp = tb("nexp", [P, KT])
        xw = tb("xw", [P, S, NT, D])
        vrow = tb("vrow", [P, KT])
        ohR, ohRn = tb("ohR", [P, 2, CH, P], BF16), tb("ohRn", [P, 2, CH, P], BF16)
        ohK, ohKf = tb("ohK", [P, 2, CH, KT], BF16), tb("ohKf", [P, 2, CH, KT], BF16)
        psA = c.enter_context(nc.psum_tensor(f"psA_{layer}", [P, BANK], F32))
        psB = c.enter_context(nc.psum_tensor(f"psB_{layer}", [P, BANK], F32))
        psR = c.enter_context(nc.psum_tensor(f"psR_{layer}", [P, BANK], F32))
        sem = lambda n: c.enter_context(nc.semaphore(f"{n}_{layer}"))
        gap, expd, w_ready, xw_ready, xw_stored, chosen_ready, ranked, tile_hot, row_hot, rown_hot, hot, used = map(
            sem, "gap expd w_ready xw_ready xw_stored chosen_ready ranked tile_hot row_hot rown_hot hot used".split())
        block = c.enter_context(nc.Block())

        @block.tensor
        def _(pe):
            pe.wait_ge(chosen_ready, 1)
            flat = chosen[:, :, :].rearrange("p e i -> p (e i)")
            nc.tensor.matmul(psA[:, 0:E * NT], W["before"][:, :], flat, start=True, stop=True)
            nc.tensor.matmul(psB[:, 0:E * NT], W["ones"][:, :], flat, start=True, stop=True).then_inc(ranked, 1)
            for ch in range(NCH):
                pe.wait_ge(hot, ch + 1)
                pe.wait_ge(rown_hot, ch + 1)
                for j in range(CH):
                    nc.tensor.matmul(psR[:, 0:KT], ohR[:, ch % 2, j, :], ohKf[:, ch % 2, j, :],
                                     start=(ch == 0 and j == 0), stop=False)
                    last = nc.tensor.matmul(psR[:, 0:KT], ohRn[:, ch % 2, j, :], ohK[:, ch % 2, j, :],
                                            start=False, stop=(ch == NCH - 1 and j == CH - 1))
                last.then_inc(used, 1)

        @block.scalar
        def _(act):
            act.wait_ge(gap, 1)
            nc.scalar.activation(m[1][:, :], m[1][:, :], ACT.Exp).then_inc(expd, 1)
            act.wait_ge(w_ready, 1)
            early = 3 * S * NT // 8
            each = (S * NT - early) // NCH

            def weigh(a, b):
                for s, i in [divmod(k, NT) for k in range(a, b)]:
                    nc.scalar.activation(xw[:, s, i, :], XN[:, i, :], ACT.Copy,
                                         scale=w[:, s, i:i + 1]).then_inc(xw_ready, 1)

            weigh(0, early)
            for ch in range(NCH):
                act.wait_ge(row_hot, ch + 1)
                if ch >= 2:
                    act.wait_ge(used, ch - 1)
                nc.scalar.activation(ohRn[:, ch % 2, :, :], ohR[:, ch % 2, :, :], ACT.Copy,
                                     scale=W["rowno"][:, :]).then_inc(rown_hot, 1)
                weigh(early + ch * each, early + (ch + 1) * each)

        @block.sync
        def _(sp):
            rows = W["xw_dram"].rearrange("(s i p) d -> p s i d", s=S, p=P)
            for s in range(S):
                for b in range(SEQS):
                    at = slice(TS * b, TS * (b + 1))
                    sp.wait_ge(xw_ready, s * NT + TS * (b + 1))
                    sp.dma_start(rows[:, s, at, :], xw[:, s, at, :]).then_inc(xw_stored, 16)
            sp.wait_ge(xw_stored, 16 * S * SEQS)

        if layer == 0:
            @block.gpsimd
            def _(pool):
                nc.gpsimd.memset(W["pick"][:, :, :], 0.0).then_inc(W["pick_made"], 1)
                for g in range(3):
                    pool.wait_ge(W["pick_made"], 1 + g)
                    rows = W["pick"][g * 2 * N:(g + 1) * 2 * N, :, :]
                    nc.gpsimd.affine_select(out=rows, in_=rows, compare_op=ALU.not_equal, fill=1.0, base=0,
                                            pattern=[[-1, 2 * N], [0, P]],
                                            channel_multiplier=1).then_inc(W["pick_made"], 1)

        @block.vector
        def _(dve):
            link = linker(dve, W)
            v = nc.vector

            def over_e(t):
                return t.unsqueeze(2).to_broadcast([P, NT, E])
            revB = rev[:, :].unsqueeze(1).to_broadcast([P, NT, E])
            if layer == 0:
                dve.wait_ge(W["small_came"], 16 * SMALL)
            link(v.tensor_tensor(lg[:, :, :], psL[:, 0:NT * E].rearrange("p (i e) -> p i e", e=E),
                                 W["bgB"][:, :].unsqueeze(1).to_broadcast([P, NT, E]), ALU.add))
            for s in range(S):
                link(v.reduce_max(m[s][:, :], lg[:, :, :], axis=AX.X))
                link(v.tensor_tensor(tmp[:, :, :], lg[:, :, :], over_e(m[s][:, :]), ALU.is_ge))
                link(v.tensor_tensor(tmp[:, :, :], tmp[:, :, :], revB, ALU.mult))
                link(v.reduce_max(mq[:, :], tmp[:, :, :], axis=AX.X))
                link(v.tensor_tensor(oh[s][:, :, :], revB, over_e(mq[:, :]), ALU.is_equal))
                if s == 0:
                    link(v.scalar_tensor_tensor(lg[:, :, :], oh[0][:, :, :], -BIG, lg[:, :, :],
                                                ALU.mult, ALU.add))
            v.tensor_tensor(chosen[:, :, :].rearrange("p e i -> p i e"), oh[0][:, :, :], oh[1][:, :, :],
                            ALU.add).then_inc(chosen_ready, 1)
            v.tensor_tensor(m[1][:, :], m[1][:, :], m[0][:, :], ALU.subtract).then_inc(gap, 1)
            dve.wait_ge(expd, 1)
            link(v.tensor_scalar(mq[:, :], m[1][:, :], 1.0, None, ALU.add))
            link(v.reciprocal(w[:, 0, :], mq[:, :]))
            v.tensor_tensor(w[:, 1, :], w[:, 0, :], m[1][:, :], ALU.mult).then_inc(w_ready, 1)
            dve.wait_ge(ranked, 1)
            flat = lambda t: t[:, :, :].rearrange("p e i -> p (e i)")
            link(v.tensor_copy(flat(tot), psB[:, 0:E * NT]))
            link(v.tensor_tensor_scan(flat(inc), flat(W["notfirst"]), flat(tot), 0.0, ALU.mult, ALU.add))
            link(v.tensor_tensor(flat(pos), flat(inc), flat(tot), ALU.subtract))
            link(v.tensor_tensor(flat(pos), flat(pos), psA[:, 0:E * NT], ALU.add))
            link(v.tensor_scalar(cnt[:, :], inc[:, :, NT - 1], float(P - 1), None, ALU.add))
            link(v.tensor_single_scalar(cnt[:, :], cnt[:, :], 7, ALU.arith_shift_right))
            link(v.tensor_copy(tiles[:, :], cnt[:, :]))
            link(v.tensor_tensor_scan(tend[:, :], W["ones"][:, 0:E], tiles[:, :], 0.0, ALU.mult, ALU.add))
            link(v.tensor_tensor(toff[:, :], tend[:, :], tiles[:, :], ALU.subtract))
            link(v.tensor_scalar(toff[:, :], toff[:, :], float(P), None, ALU.mult))
            link(v.tensor_tensor(pos[:, :, :], pos[:, :, :],
                                 toff[:, :].unsqueeze(2).to_broadcast([P, E, NT]), ALU.add))
            for s in range(S):
                link(v.tensor_tensor(tmp[:, :, :], oh[s][:, :, :],
                                     pos[:, :, :].rearrange("p e i -> p i e"), ALU.mult))
                link(v.reduce_sum(ppos[:, s, :], tmp[:, :, :], axis=AX.X))
            link(v.tensor_copy(pint[:, :, :], ppos[:, :, :]))
            link(v.tensor_single_scalar(pint[:, :, :], pint[:, :, :], 7, ALU.arith_shift_right))
            link(v.tensor_copy(pk[:, :, :], pint[:, :, :]))
            link(v.scalar_tensor_tensor(pr[:, :, :], pk[:, :, :], -float(P), ppos[:, :, :], ALU.mult, ALU.add))
            for ch in range(NCH):
                s, i0 = ch // (NT // CH), ch % (NT // CH) * CH
                if ch >= 2:
                    dve.wait_ge(used, ch - 1)
                col = lambda t: t[:, s, i0:i0 + CH].unsqueeze(2)
                iK = W["iotaK"][:, :].unsqueeze(1).to_broadcast([P, CH, KT])
                o = ohK[:, ch % 2, :, :]
                of = ohKf[:, ch % 2, :, :]
                v.tensor_tensor(o, iK, col(pk).to_broadcast([P, CH, KT]), ALU.is_equal).then_inc(tile_hot, 1)
                v.tensor_tensor(ohR[:, ch % 2, :, :], W["iotaR"][:, :].unsqueeze(1).to_broadcast([P, CH, P]),
                                col(pr).to_broadcast([P, CH, P]), ALU.is_equal).then_inc(row_hot, 1)
                dve.wait_ge(tile_hot, ch + 1)
                v.tensor_tensor(of, o, col(first).to_broadcast([P, CH, KT]), ALU.mult).then_inc(hot, 1)
            link(v.tensor_tensor(past[:, :, :], W["iotaK"][:, :].unsqueeze(2).to_broadcast([P, KT, E]),
                                 tend[:, :].unsqueeze(1).to_broadcast([P, KT, E]), ALU.is_ge))
            link(v.reduce_sum(nexp[:, :], past[:, :, :], axis=AX.X))
            v.tensor_scalar(W["expertW"][:, :], nexp[:, :], float(E - 1), None, ALU.min)
            dve.wait_ge(used, NCH)
            link(v.scalar_tensor_tensor(vrow[:, :], psR[:, 0:KT], 0.0, W["padrow"][:, :], ALU.is_equal, ALU.mult))
            link(v.scalar_tensor_tensor(W["rowY"][:, :], psR[:, 0:KT], -1.0, vrow[:, :], ALU.add, ALU.add))
            link(v.tensor_single_scalar(W["rowG"][:, :], W["rowY"][:, :], S * T - 1, ALU.bitwise_and))


def experts(nc, W, layer):
    J = 8
    LAG = 2
    AHEAD = 2
    XCOLS = NT // (2 * J)
    X, XN = W["X"], W["XN"]
    rowG, rowY, expertW = W["rowG"], W["rowY"], W["expertW"]
    with ExitStack() as c:
        tb = lambda n, shape, dt=F32: c.enter_context(nc.sbuf_tensor(f"{n}_{layer}", shape, dt))
        ps = lambda n: c.enter_context(nc.psum_tensor(f"{n}_{layer}", [P, BANK], F32))
        sem = lambda n: c.enter_context(nc.semaphore(f"{n}_{layer}"))
        xg = [tb(f"xg{j}", [P, D]) for j in range(J)]
        xTh = [tb(f"xTh{j}", [D, P], F32R) for j in range(2)]
        xTl = [tb(f"xTl{j}", [D, P], F32R) for j in range(2)]
        sg = [tb(f"sg{j}", [P, H]) for j in range(2)]
        hid = [tb(f"hid{j}", [P, H]) for j in range(2)]
        hT = [tb(f"hT{j}", [P, H]) for j in range(2)]
        yb = [tb(f"yb{j}", [P, D]) for j in range(J)]
        colG = [tb(f"colG{j}", [P, 1], I32) for j in range(J)]
        colY = [tb(f"colY{j}", [P, 1], I32) for j in range(J)]
        psX, psH = ps("psX"), ps("psH")
        passed = W["passed"]
        psG = [ps(f"psG{j}") for j in range(2)]
        psU = [ps(f"psU{j}") for j in range(2)]
        psY = [ps(f"psY{j}") for j in range(2)]
        gathered, scattered = W["gathered"], W["scattered"]
        before = layer * 16 * (KT // J)
        gcol, ycol, x_turned, x_high, x_low, up_g, up_u, silu_ready, hid_ready, h_turned, h_copied, \
            y_ready, y_copied = map(sem, ("gcol ycol x_turned x_high x_low up_g up_u silu_ready hid_ready "
                                          "h_turned h_copied y_ready y_copied").split())
        block = c.enter_context(nc.Block())

        def column(t, k):
            return t[:, bass.ds(k, 1)]

        def turns(eng, step, first, end):
            with eng.Fori(first, end) as turn:
                for j in range(J):
                    step(turn * J + j, j)

        def wait(eng, sem_, k, back):
            if not isinstance(k, int) or k - back >= 0:
                eng.wait_ge(sem_, k - back + 1)

        @block.gpsimd
        def _(pool):
            def gather(k, j):
                wait(pool, x_turned, k, J)
                nc.gpsimd.tensor_copy(colG[j][:, :], column(rowG, k)).then_inc(gcol, 1)
                pool.wait_ge(gcol, k + 1)
                pool.sem_inc(passed, 1)
                nc.gpsimd.indirect_dma_start(
                    xg[j][:, :], None, W["xw_dram"], bass.IndirectOffsetOnAxis(ap=colG[j][:, :], axis=0)
                ).then_inc(gathered[j], 16)

            def scatter(k, j):
                wait(pool, y_copied, k, 0)
                nc.gpsimd.tensor_copy(colY[j][:, :], column(rowY, k)).then_inc(ycol, 1)
                pool.wait_ge(ycol, k + 1)
                pool.sem_inc(passed, 1)
                nc.gpsimd.indirect_dma_start(
                    W["y_dram"], bass.IndirectOffsetOnAxis(ap=colY[j][:, :], axis=0), yb[j][:, :], None
                ).then_inc(scattered[j], 16)

            def step(k, j):
                if not isinstance(k, int) or k >= J:
                    scatter(k - J, j)
                gather(k, j)
            for k in range(J):
                step(k, k)
            turns(pool, step, 1, KT // J)
            for k in range(KT - J, KT):
                scatter(k, k % J)
            for j in range(J):
                pool.wait_ge(scattered[j], before + 16 * (KT // J))

        @block.vector
        def _(dve):
            def rest_x(k, j):
                wait(dve, x_high, k, 0)
                wait(dve, up_u, k, 2)
                nc.vector.tensor_tensor(xTl[j % 2][:, :], psX[:, 0:P], xTh[j % 2][:, :],
                                        ALU.subtract).then_inc(x_low, 1)

            def multiply(k, j):
                wait(dve, silu_ready, k, 0)
                wait(dve, up_u, k, 0)
                wait(dve, h_turned, k, 2)
                nc.vector.tensor_tensor(hid[j % 2][:, :], sg[j % 2][:, :], psU[j % 2][:, :],
                                        ALU.mult).then_inc(hid_ready, 1)

            def take_y(k, j, turn):
                wait(dve, y_ready, k, 0)
                if not isinstance(k, int) or k >= J:
                    dve.wait_ge(scattered[j], turn * 16 + before)
                nc.vector.tensor_copy(yb[j][:, :], psY[j % 2][:, 0:D]).then_inc(y_copied, 1)

            rest_x(0, 0)
            rest_x(1, 1)
            for k in range(2 * J):
                multiply(k, k % J)
                rest_x(k + AHEAD, (k + AHEAD) % J)
                if k >= LAG:
                    take_y(k - LAG, (k - LAG) % J, (k - LAG) // J)
                at = slice(k * XCOLS, (k + 1) * XCOLS)
                nc.vector.scalar_tensor_tensor(X[:, at, :], XN[:, at, :], 0.5, X[:, at, :], ALU.mult, ALU.add)
            with dve.Fori(2, KT // J - 1) as turn:
                for j in range(J):
                    k = turn * J + j
                    multiply(k, j)
                    rest_x(k + AHEAD, (j + AHEAD) % J)
                    take_y(k - LAG, (j - LAG) % J, turn + (j - LAG) // J)
            for k in range(KT - J, KT + LAG):
                if k < KT:
                    multiply(k, k % J)
                if k + AHEAD < KT:
                    rest_x(k + AHEAD, (k + AHEAD) % J)
                take_y(k - LAG, (k - LAG) % J, (k - LAG) // J)

        @block.scalar
        def _(act):
            def copy_x(k, j):
                wait(act, x_turned, k, 0)
                wait(act, up_u, k, 2)
                nc.scalar.activation(xTh[j % 2][:, :], psX[:, 0:P], ACT.Copy).then_inc(x_high, 1)

            def silu(k, j):
                wait(act, up_g, k, 0)
                wait(act, hid_ready, k, 2)
                nc.scalar.activation(sg[j % 2][:, :], psG[j % 2][:, :], ACT.Silu).then_inc(silu_ready, 1)

            def copy_h(k, j):
                wait(act, h_turned, k, 0)
                wait(act, y_ready, k, 2)
                nc.scalar.activation(hT[j % 2][:, :], psH[:, :], ACT.Copy).then_inc(h_copied, 1)

            def step(k, j):
                inside = not isinstance(k, int)
                if inside or k < KT:
                    silu(k, j)
                if inside or k + AHEAD < KT:
                    copy_x(k + AHEAD, j)
                if inside or k >= 1:
                    copy_h(k - 1, j + 1)
            copy_x(0, 0)
            copy_x(1, 1)
            for k in range(J):
                step(k, k % J)
            turns(act, step, 1, KT // J - 1)
            for k in range(KT - J, KT + 1):
                step(k, k)

        @block.tensor
        def _(pe):
            def turn_x(k, j, turn):
                pe.wait_ge(gathered[j], turn * 16 + (before + 16))
                wait(pe, x_low, k, 1)
                nc.tensor.transpose(psX[:, 0:P], xg[j][:, :], W["ident"][:, :]).then_inc(x_turned, 1)

            def expert(k):
                return pe.value_load(expertW[0:1, bass.ds(k, 1)], min_val=0, max_val=E - 1)

            def up(k, j, e):
                wait(pe, x_high, k, 0)
                wait(pe, silu_ready, k, 2)
                wait(pe, hid_ready, k, 2)
                at = bass.ds(e * H, H)
                high, low, g, u = xTh[j % 2][:, :], xTl[j % 2][:, :], psG[j % 2][:, :], psU[j % 2][:, :]
                nc.tensor.matmul(g, high, W["W1h"][:, at], start=True, stop=False)
                nc.tensor.matmul(g, high, W["W1l"][:, at], start=False, stop=False)
                nc.tensor.matmul(u, high, W["W3h"][:, at], start=True, stop=False)
                nc.tensor.matmul(u, high, W["W3l"][:, at], start=False, stop=False)
                wait(pe, x_low, k, 0)
                nc.tensor.matmul(g, low, W["W1h"][:, at], start=False, stop=True).then_inc(up_g, 1)
                nc.tensor.matmul(u, low, W["W3h"][:, at], start=False, stop=True).then_inc(up_u, 1)

            def turn_h(k, j):
                wait(pe, hid_ready, k, 0)
                wait(pe, h_copied, k, 1)
                for q in range(HC):
                    last = nc.tensor.transpose(psH[:, q * P:(q + 1) * P], hid[j % 2][:, q * P:(q + 1) * P],
                                               W["ident"][:, :])
                last.then_inc(h_turned, 1)

            def down(k, j, e):
                wait(pe, h_copied, k, 0)
                wait(pe, y_copied, k, 2)
                for q in range(HC):
                    last = nc.tensor.matmul(psY[j % 2][:, 0:D], hT[j % 2][:, q * P:(q + 1) * P],
                                            W["W2s"][:, bass.ds(e * (HC * D) + q * D, D)],
                                            start=(q == 0), stop=(q == HC - 1))
                last.then_inc(y_ready, 1)

            def steps_of(tiles, turn):
                e = {0: expert(tiles[0][0])}
                for at, (k, j) in enumerate(tiles):
                    inside = not isinstance(k, int)
                    if inside or k < KT:
                        up(k, j, e[at])
                    if inside or k + AHEAD < KT:
                        turn_x(k + AHEAD, (j + AHEAD) % J, turn + (j + AHEAD) // J)
                    if at + 1 < len(tiles) and (inside or k + 1 < KT):
                        e[at + 1] = expert(tiles[at + 1][0])
                    if inside or 1 <= k <= KT:
                        turn_h(k - 1, j + 1)
                    if inside or k >= LAG:
                        down(k - LAG, j, e[at - LAG] if at >= LAG else expert(k - LAG))

            if layer == 0:
                pe.wait_ge(W["w2_came"], 16)
            turn_x(0, 0, 0)
            turn_x(1, 1, 0)
            steps_of([(k, k) for k in range(2 * J)], 0)
            with pe.Fori(1, KT // (2 * J)) as turn:
                steps_of([(turn * (2 * J) + j, j) for j in range(2 * J)], turn * 2)
            steps_of([(k, k - (KT - J)) for k in range(KT - J, KT + LAG)], KT // J - 1)


def combine(nc, W):
    X = W["X"]
    with ExitStack() as c:
        ya = c.enter_context(nc.sbuf_tensor("ya", [P, S, NT, D], F32))
        sem = lambda n: c.enter_context(nc.semaphore(n))
        sent = sem("sent")
        block = c.enter_context(nc.Block())
        W["summed_from"] = W["own_steps"]

        @block.vector
        def _(dve):
            link = linker(dve, W)
            for b in range(SEQS):
                add_outputs(nc, dve, link, W, ya, b)

        @block.sync
        def _(sp):
            load_outputs(sp, W, ya)
            res = W["out"].rearrange("b (i p) d -> p (b i) d", p=P)
            for b in range(SEQS):
                at = slice(TS * b, TS * (b + 1))
                sp.wait_ge(W["own_step"], W["summed_from"] + 2 * (b + 1))
                sp.dma_start(res[:, at, :], X[:, at, :]).then_inc(sent, 16)
            sp.wait_ge(sent, 16 * SEQS)


def steps(nc, W):
    XT, DT, BC3 = W["XT"], W["DT"], W["BC3"]
    C = 2 * N
    RB = 3
    per = BANK // P
    with ExitStack() as c:
        tb = lambda n, shape: c.enter_context(nc.sbuf_tensor(n, shape, F32))
        ps = lambda n: c.enter_context(nc.psum_tensor(n, [P, BANK], F32))
        sem = lambda n: c.enter_context(nc.semaphore(n))
        rT = [tb(f"rT{j}", [R, BANK]) for j in range(2)]
        bc = [tb(f"bc{j}", [C, BANK]) for j in range(RB)]
        packed = tb("packed", [SEQS * C, L])
        parts = [c.enter_context(nc.sbuf_tensor(f"part{j}", [SEQS * C, L], BF16)) for j in range(3)]
        u = tb("u", [D, T])
        lost = [tb(f"lost{j}", [D, BANK]) for j in range(2)]
        psBt = ps("psBt")
        psr = [ps(f"psr{j}") for j in range(2)]
        psz = [ps(f"psz{j}") for j in range(2)]
        psbc = [ps(f"psbc{j}") for j in range(2)]
        low, low_c, bc_done, bc_taken, z_done, abs_ready, relu_ready, u_ready, ln_ready, \
            part_ready, rest_ready, parts_stored, g_ready, lost_ready, base_ready, added, b_turned = map(
                sem, ("low low_c bc_done bc_taken z_done abs_ready relu_ready u_ready ln_ready "
                      "part_ready rest_ready parts_stored g_ready lost_ready base_ready added b_turned").split())
        block = c.enter_context(nc.Block())
        cut = lambda t, q: t[:, q * BANK:(q + 1) * BANK]
        bc_packed = W["bc_packed"]

        @block.sync
        def _(sp):
            for q in range(QN):
                b, half = q // 2, q % 2
                sp.wait_ge(bc_taken, q + 1)
                sp.dma_start(packed[b * C:(b + 1) * C, half * BANK:(half + 1) * BANK],
                             bc[q % RB][:, :]).then_inc(bc_packed[q % RB], 16)
            for j in range(3):
                sp.wait_ge(part_ready, j + 1)
                for b in range(SEQS):
                    sp.dma_start(BC3[(2 - j) * C:(3 - j) * C, b * L:(b + 1) * L],
                                 parts[j][b * C:(b + 1) * C, :]).then_inc(parts_stored, 16)
            sp.wait_ge(parts_stored, 16 * 3 * SEQS)

        @block.tensor
        def _(pe):
            def project_bc(q):
                if q >= 2:
                    pe.wait_ge(bc_taken, q - 1)
                nc.tensor.matmul(psbc[q % 2][0:C, :], W["W_ins"][:, :], cut(XT, q), start=True,
                                 stop=True).then_inc(bc_done, 1)

            def turn_b(q):
                pe.wait_ge(bc_taken, q + 1)
                for i in range(per):
                    at = (q * per + i) * N
                    last = nc.tensor.transpose(psBt[:, at:at + N], bc[q % RB][0:N, i * P:(i + 1) * P],
                                               W["ident"][0:N, 0:N])
                last.then_inc(b_turned, 1)

            for q in range(QN + 1):
                if q < QN:
                    if q >= 2:
                        pe.wait_ge(low_c, q - 1)
                    nc.tensor.matmul(psr[q % 2][0:R, :], W["W_dt1s"][:, :], cut(XT, q), start=True,
                                     stop=True).then_inc(low, 1)
                if 2 * q < QN:
                    project_bc(2 * q)
                    project_bc(2 * q + 1)
                if q >= 1:
                    z = q - 1
                    if 2 * z < QN:
                        turn_b(2 * z)
                        turn_b(2 * z + 1)
                    pe.wait_ge(low_c, z + 1)
                    if z >= 2:
                        pe.wait_ge(relu_ready, z - 1)
                    nc.tensor.matmul(psz[z % 2][:, :], W["W_dt2s"][:, :], rT[z % 2][:, :],
                                     start=True, stop=True).then_inc(z_done, 1)

        @block.scalar
        def _(act):
            def take_bc(q):
                act.wait_ge(bc_done, q + 1)
                if q >= RB:
                    act.wait_ge(bc_packed[q % RB], 16 * (q // RB))
                    act.wait_ge(b_turned, q - RB + 1)
                nc.scalar.activation(bc[q % RB][:, :], psbc[q % 2][0:C, :], ACT.Identity,
                                     bias=W["b_inc"][:, :]).then_inc(bc_taken, 1)

            for q in range(QN + 1):
                z = q - 1
                if q < QN:
                    act.wait_ge(low, q + 1)
                    if q >= 2:
                        act.wait_ge(z_done, q - 1)
                    nc.scalar.activation(rT[q % 2][:, :], psr[q % 2][0:R, :], ACT.Identity,
                                         bias=W["b_dt1c"][:, :]).then_inc(low_c, 1)
                if 2 * q < QN:
                    take_bc(2 * q)
                    take_bc(2 * q + 1)
                if q >= 1:
                    act.wait_ge(z_done, z + 1)
                    nc.scalar.activation(cut(u, z), psz[z % 2][:, :], ACT.Abs,
                                         bias=W["b_dt2c"][:, :]).then_inc(abs_ready, 1)
                    act.wait_ge(abs_ready, z + 1)
                    nc.scalar.activation(cut(u, z), cut(u, z), ACT.Exp, scale=-1.0).then_inc(u_ready, 1)
            act.wait_ge(b_turned, QN)
            nc.scalar.activation(W["Btok"][:, :, :].rearrange("p i n -> p (i n)"), psBt[:, :], ACT.Copy)
            for q in range(QN):
                act.wait_ge(lost_ready, q + 1)
                nc.scalar.activation(cut(u, q), cut(u, q), ACT.Ln, bias=1.0).then_inc(ln_ready, 1)

        @block.gpsimd
        def _(pool):
            def rest(j):
                pool.wait_ge(part_ready, j + 1)
                nc.gpsimd.tensor_tensor(packed[:, :], packed[:, :], parts[j][:, :],
                                        ALU.subtract).then_inc(rest_ready, 1)

            for z in range(QN):
                if z in (4, 6):
                    rest(z // 2 - 2)
                pool.wait_ge(g_ready, z + 1)
                nc.gpsimd.tensor_tensor(lost[z % 2][:, :], cut(u, z), lost[z % 2][:, :],
                                        ALU.subtract).then_inc(lost_ready, 1)

        @block.vector
        def _(dve):
            v = nc.vector
            v.tensor_scalar(W["Ahalf"][:, :], W["As"][:, :], 0.5, None, ALU.mult)
            v.reciprocal(W["Ainv"][:, :], W["As"][:, :])

            def part(j):
                if j == 0:
                    for k in range(RB):
                        dve.wait_ge(bc_packed[k], 16 * len(range(k, QN, RB)))
                else:
                    dve.wait_ge(rest_ready, j)
                v.tensor_copy(parts[j][:, :], packed[:, :]).then_inc(part_ready, 1)

            for q in range(1, QN + 3):
                if q <= QN:
                    z = q - 1
                    dve.wait_ge(abs_ready, z + 1)
                    v.tensor_scalar(cut(DT, z), psz[z % 2][:, :], W["b_dt2c"][:, :], 0.0, ALU.add,
                                    ALU.max).then_inc(relu_ready, 1)
                if 2 <= q <= QN + 1:
                    z = q - 2
                    dve.wait_ge(u_ready, z + 1)
                    if z >= 2:
                        dve.wait_ge(base_ready, z - 1)
                    v.tensor_scalar(lost[z % 2][:, :], cut(u, z), 1.0, -1.0, ALU.add, ALU.add).then_inc(g_ready, 1)
                if q >= 3:
                    z = q - 3
                    dve.wait_ge(lost_ready, z + 1)
                    v.tensor_tensor(cut(DT, z), cut(DT, z), lost[z % 2][:, :], ALU.add).then_inc(base_ready, 1)
                if q in (5, 7, 9):
                    part((q - 5) // 2)
            for q in range(QN + 1):
                if q < QN:
                    dve.wait_ge(base_ready, q + 1)
                    dve.wait_ge(ln_ready, q + 1)
                    v.tensor_tensor(cut(DT, q), cut(DT, q), cut(u, q), ALU.add).then_inc(added, 1)
                if q >= 1:
                    dve.wait_ge(added, q)
                    v.tensor_scalar(cut(DT, q - 1), cut(DT, q - 1), DT_MIN, DT_MAX, ALU.max, ALU.min)


def scan(nc, W):
    XT, DT, BC3 = W["XT"], W["DT"], W["BC3"]
    UN = T // BANK
    RING = 4
    PIECES = L // BANK
    BX_DVE = (7,)
    BX_TURN = (1, 5, 9, 13)
    BX_ACT = [n for n in range(N) if n not in BX_DVE]
    BX_POOL = [n for n in BX_ACT if n not in BX_TURN]
    PT = BANK // P
    with ExitStack() as c:
        tb = lambda n, shape, dt=F32: c.enter_context(nc.sbuf_tensor(n, shape, dt))
        ps = lambda n: c.enter_context(nc.psum_tensor(n, [P, BANK], F32))
        sem = lambda n: c.enter_context(nc.semaphore(n))
        pick, passed = W["pick"], W["passed"]
        th = [tb(f"th{j}", [D, BANK]) for j in range(RING)]
        bsb = [tb(f"bsb{j}", [D, BANK]) for j in range(2)]
        xb = tb("xb", [P, BANK])
        bxs = [tb(f"bxs{j}", [D, BANK]) for j in range(RING)]
        drv = [tb(f"drv{j}", [D, BANK]) for j in range(2)]
        h = [tb(f"h{j}", [D, BANK]) for j in range(2)]
        hc = [tb(f"hc{j}", [D, BANK]) for j in range(RING)]
        start = tb("start", [D, PIECES, N])
        abar = [ps(f"abar{j}") for j in range(RING)]
        psB, psY = ps("psBs"), ps("psYs")
        psC = [ps(f"psCs{j}") for j in range(2)]
        start_clear, b_there, b_kept, c_there, c_used, decayed, halved, h_kept, driven, bx_pool, bx_dve, xb_there, expm1_there, \
            recurred, c_summed, y_taken = map(
                sem, ("start_clear b_there b_kept c_there c_used decayed halved h_kept driven bx_pool "
                      "bx_dve xb_there expm1_there recurred c_summed y_taken").split())
        block = c.enter_context(nc.Block())

        def walk(*ops):
            def piece(u):
                for n in range(N):
                    for lead, op in ops:
                        du, dn = divmod(n + lead, N)
                        if not isinstance(u, int) or 0 <= u + du < UN:
                            op(u + du, dn)
            return piece

        def run(eng, *ops):
            piece = walk(*ops)
            for lead in range(6, 0, -1):
                for its, op in ops:
                    if its >= lead:
                        op(0, its - lead)
            piece(0)
            with eng.Fori(1, UN - 1) as u:
                piece(u)
            piece(UN - 1)
            for n in range(4):
                for lead, op in ops:
                    if n + lead < 0:
                        op(UN - 1, N + n + lead)

        def wait(eng, sem_, u, n, back=0, states=range(N)):
            du, dn = divmod(n - back, N)
            more = du * len(states) + len([k for k in states if k <= dn])
            if not isinstance(u, int) or u * len(states) + more > 0:
                eng.wait_ge(sem_, u * len(states) + more)

        def wait_bx(eng, u, n):
            if n in BX_DVE:
                wait(eng, bx_dve, u, n, 0, BX_DVE)
            elif n in BX_TURN:
                wait(eng, b_kept, u, n, 0, BX_ACT)
            else:
                wait(eng, bx_pool, u, n, 0, BX_POOL)

        def later(u):
            return not isinstance(u, int) or u > 0

        def cols(t, u):
            return t[:, bass.ds(u * BANK, BANK)]

        @block.tensor
        def _(pe):
            def spread_b(u, n):
                if (n - 1) % N in BX_DVE:
                    wait(pe, bx_dve, u, n, 1, BX_DVE)
                else:
                    wait(pe, b_kept, u, n, 1, BX_ACT)
                if n in BX_TURN:
                    wait(pe, xb_there, u, n, 0, BX_TURN)
                    for i in range(PT):
                        last = nc.tensor.transpose(psB[:, i * P:(i + 1) * P], xb[:, i * P:(i + 1) * P],
                                                   W["ident"][:, :])
                    last.then_inc(b_there, 1)
                    return
                nc.tensor.matmul(psB[:, :], pick[:, n, :], cols(BC3, u), start=True, stop=True).then_inc(b_there, 1)

            def spread_c(u, n):
                wait(pe, c_used, u, n, 2)
                nc.tensor.matmul(psC[n % 2][:, :], pick[:, N + n, :], cols(BC3, u), start=True,
                                 stop=True).then_inc(c_there, 1)

            def sum_c(u, n):
                wait(pe, c_used, u, n)
                if n == 0 and later(u):
                    pe.wait_ge(y_taken, u)
                nc.tensor.matmul(psY[:, :], W["ident"][:, :], hc[n % RING][:, :], start=(n == 0),
                                 stop=(n == N - 1)).then_inc(c_summed, 1)

            run(pe, (5, spread_b), (1, spread_c), (-2, sum_c))

        @block.scalar
        def _(act):
            def keep_h(u, n):
                wait(act, recurred, u, n)
                nc.scalar.activation(start[:, 1, n:n + 1], h[n % 2][:, BANK - 1:BANK], ACT.Copy).then_inc(h_kept, 1)

            def decay(u, n):
                wait(act, recurred, u, n, RING)
                wait(act, driven, u, n, RING)
                act.sem_inc(passed, 1)
                nc.scalar.activation(abar[n % RING][:, :], cols(DT, u), ACT.Exp,
                                     scale=W["As"][:, n:n + 1]).then_inc(decayed, 1)
                nc.scalar.activation(th[n % RING][:, :], cols(DT, u), ACT.Tanh,
                                     scale=W["Ahalf"][:, n:n + 1]).then_inc(halved, 1)

            def keep_b(u, n):
                if n not in BX_ACT:
                    return
                wait(act, b_there, u, n)
                if n in BX_TURN:
                    wait(act, driven, u, n, RING)
                    nc.scalar.activation(bxs[n % RING][:, :], psB[:, :], ACT.Copy).then_inc(b_kept, 1)
                    return
                wait(act, bx_pool, u, n, 2, BX_POOL)
                nc.scalar.activation(bsb[n % 2][:, :], psB[:, :], ACT.Copy).then_inc(b_kept, 1)

            def rows_bx(u, n):
                if n not in BX_TURN:
                    return
                wait(act, b_there, u, n, 4)
                act.sem_inc(passed, 1)
                for i in range(PT):
                    at = bass.ds(u * PT + i, 1)
                    last = nc.scalar.activation(xb[:, i * P:(i + 1) * P],
                                                W["XN"][:, at, :].rearrange("p i d -> p (i d)"), ACT.Copy,
                                                scale=W["Btok"][:, at, n:n + 1].rearrange("p i n -> p (i n)"))
                last.then_inc(xb_there, 1)

            run(act, (-1, keep_h), (3, decay), (6, rows_bx), (4, keep_b))

        @block.gpsimd
        def _(pool):
            def drive(u, n):
                wait(pool, expm1_there, u, n)
                wait_bx(pool, u, n)
                wait(pool, recurred, u, n, 2)
                nc.gpsimd.tensor_tensor(drv[n % 2][:, :], th[n % RING][:, :], bxs[n % RING][:, :],
                                        ALU.mult).then_inc(driven, 1)

            def bx(u, n):
                if n not in BX_POOL:
                    return
                wait(pool, b_kept, u, n, 0, BX_ACT)
                wait(pool, driven, u, n, RING)
                pool.sem_inc(passed, 1)
                nc.gpsimd.tensor_tensor(bxs[n % RING][:, :], bsb[n % 2][:, :], cols(XT, u),
                                        ALU.mult).then_inc(bx_pool, 1)

            run(pool, (1, drive), (3, bx))

        @block.vector
        def _(dve):
            v = nc.vector

            def expm1(u, n):
                wait(dve, decayed, u, n)
                wait(dve, halved, u, n)
                v.scalar_tensor_tensor(th[n % RING][:, :], abar[n % RING][:, :], 1.0, th[n % RING][:, :], ALU.add,
                                       ALU.mult).then_inc(expm1_there, 1)

            def bx(u, n):
                if n not in BX_DVE:
                    return
                wait(dve, b_there, u, n)
                wait(dve, driven, u, n, RING)
                v.tensor_tensor(bxs[n % RING][:, :], psB[:, :], cols(XT, u), ALU.mult).then_inc(bx_dve, 1)

            def recur(u, n):
                wait(dve, driven, u, n)
                wait(dve, c_used, u, n, 2)
                wait(dve, h_kept, u, n, 2)
                v.tensor_tensor_scan(h[n % 2][:, :], abar[n % RING][:, :], drv[n % 2][:, :],
                                     starts(u, n), ALU.mult, ALU.add).then_inc(recurred, 1)

            def starts(u, n):
                if isinstance(u, int):
                    return start[:, u % PIECES, n:n + 1]
                return start[:, bass.ds(u % PIECES, 1), n:n + 1].rearrange("d a n -> d (a n)")

            def times_c(u, n):
                wait(dve, recurred, u, n)
                wait(dve, c_there, u, n)
                wait(dve, c_summed, u, n, RING)
                v.scalar_tensor_tensor(hc[n % RING][:, :], h[n % 2][:, :], W["Ainv"][:, n:n + 1], psC[n % 2][:, :],
                                       ALU.mult, ALU.mult).then_inc(c_used, 1)

            def take_y(u, n):
                if n == N - 1:
                    wait(dve, c_summed, u, n)
                    v.scalar_tensor_tensor(cols(XT, u), cols(XT, u), W["Dc"][:, :], psY[:, :], ALU.mult,
                                           ALU.add).then_inc(y_taken, 1)

            v.memset(start[:, :, :], 0.0).then_inc(start_clear, 1)
            dve.wait_ge(start_clear, 1)
            run(dve, (2, expm1), (0, recur), (4, bx), (-1, times_c), (-3, take_y))


_INS = ['L0_attn_x', 'L0_attn_W_in', 'L0_attn_b_in', 'L0_attn_W_dt1', 'L0_attn_b_dt1', 'L0_attn_W_dt2',
        'L0_attn_b_dt2', 'L0_attn_A', 'L0_attn_D', 'L0_ffn_Wg', 'L0_ffn_bg', 'L0_ffn_W1', 'L0_ffn_W2', 'L0_ffn_W3']


def kernel(**inputs):
    import numpy as np
    import concourse.bacc as bacc
    from concourse.bass_utils import run_bass_kernel_spmd

    nc = bacc.Bacc("TRN2", target_bir_lowering=False, num_devices=1)
    arrays, args = {}, []
    for name in _INS:
        a = np.ascontiguousarray(inputs[name])
        arrays[f"in_{name}"] = a
        args.append(nc.dram_tensor(f"in_{name}", a.shape, mybir.dt.from_np(a.dtype), kind="ExternalInput").ap())
    shape = inputs['L0_attn_x'].shape
    out = nc.dram_tensor("out_x", shape, F32, kind="ExternalOutput").ap()
    macaron(nc, *args, out)
    r = run_bass_kernel_spmd(nc, [arrays], core_ids=[0])
    return r.results[0]["out_x"]
```
